# Optimizing a Trainium2 kernel written in Bass

```python
import numpy as np
import jax
import jax.numpy as jnp

def _softmax(x, axis=-1):
    return jax.nn.softmax(x, axis=axis)

def _gelu(x):
    return jax.nn.gelu(x, approximate=True)

def _silu(x):
    return jax.nn.silu(x)

def _sigmoid(x):
    return jax.nn.sigmoid(x)

def _layernorm(x, axis=-1, eps=1e-05):
    m = jnp.mean(x, axis=axis, keepdims=True)
    v = jnp.var(x, axis=axis, keepdims=True)
    return (x - m) / jnp.sqrt(v + eps)

def _scatter_add(tgt, idx, src, axis=0):
    return tgt.at[idx].add(src)

def _segment_sum(src, seg, n):
    return jax.ops.segment_sum(src, seg, n)
kernel_name = 'mk_gps_d1_gnn_r8_39b3cf'

def setup_inputs(seed: int=0):
    np.random.seed(seed)
    _w = jnp.asarray

    def _rec_inputs():
        import jax
        import jax.numpy as jnp
        _gk = jax.random.key(seed)
        x = -8.776e-05 + 1 * jax.random.normal(jax.random.fold_in(_gk, 1), (1250, 512), jnp.float32)
        src = jax.random.randint(jax.random.fold_in(_gk, 2), (20000,), 0, 1250, jnp.int32)
        dst = jnp.minimum((1250 * jax.random.uniform(jax.random.fold_in(_gk, 3), (20000,)) ** 2.0).astype(jnp.int32), 9999)
        _o = jnp.argsort(dst, stable=True)
        src = src[_o]
        dst = dst[_o]
        return (x, src, dst)
    x, src, dst = _rec_inputs()

    def _L0_gnn_setup():
        import jax, jax.numpy as jnp
        import numpy as np
        N = 1250
        E = 20000
        IN_C = 512
        HID = 512
        OUT_C = 512
        BN_EPS = 1e-05
        key = jax.random.key(seed)
        ks = jax.random.split(key, 8)
        x = jax.random.normal(ks[0], (N, IN_C), dtype=jnp.float32)
        src = jax.random.randint(ks[1], (E,), 0, N)
        off = jax.random.randint(ks[2], (E,), 1, N)
        dst = (src + off) % N
        edge_index = jnp.stack([src, dst]).astype(jnp.int64)
        W1 = jax.random.normal(ks[3], (IN_C, HID), dtype=jnp.float32) * (1.0 / np.sqrt(IN_C))
        b1 = jnp.zeros((HID,), dtype=jnp.float32)
        gamma = jnp.ones((HID,), dtype=jnp.float32)
        beta = jnp.zeros((HID,), dtype=jnp.float32)
        W2 = jax.random.normal(ks[4], (HID, OUT_C), dtype=jnp.float32) * (1.0 / np.sqrt(HID))
        b2 = jnp.zeros((OUT_C,), dtype=jnp.float32)
        return {'x': x, 'W1': W1, 'b1': b1, 'gamma': gamma, 'beta': beta, 'W2': W2, 'b2': b2, 'edge_index': edge_index}
    _L0_gnn_all = _L0_gnn_setup()
    _L0_gnn_in = {k: v for k, v in _L0_gnn_all.items() if k in ('W1', 'b1', 'gamma', 'beta', 'W2', 'b2')}
    del _L0_gnn_all

    def _L0_mix_setup():
        import jax, jax.numpy as jnp
        import numpy as np
        D_MODEL = 512
        N_HEADS = 8
        D_HEAD = D_MODEL // N_HEADS
        EPS = 1e-06

        def _split_heads(t, B, S):
            return t.reshape(B, S, N_HEADS, D_HEAD).transpose(0, 2, 1, 3)

        def _reference_tuple_inner(x, Wq, bq, Wk, bk, Wv, bv, Wo, bo):
            B, S, _ = x.shape
            q = _split_heads(x @ Wq.T + bq, B, S)
            k = _split_heads(x @ Wk.T + bk, B, S)
            v = _split_heads(x @ Wv.T + bv, B, S)
            q = jax.nn.relu(q)
            k = jax.nn.relu(k)
            k_sum = k.sum(axis=-1, keepdims=True)
            attn = jnp.einsum('bhnd,bhmd->bhnm', q, k) / (k_sum + EPS)
            attn = jax.nn.softmax(attn, axis=-1)
            out = jnp.einsum('bhnm,bhmd->bhnd', attn, v)
            out = out.transpose(0, 2, 1, 3).reshape(B, S, D_MODEL)
            return (out @ Wo.T + bo, attn)
        key = jax.random.key(seed)
        ks = jax.random.split(key, 9)
        B, S = (2, 256)
        scale = 0.02
        x = jax.random.normal(ks[0], (B, S, D_MODEL), dtype=jnp.float32)
        Wq = jax.random.normal(ks[1], (D_MODEL, D_MODEL), dtype=jnp.float32) * scale
        Wk = jax.random.normal(ks[2], (D_MODEL, D_MODEL), dtype=jnp.float32) * scale
        Wv = jax.random.normal(ks[3], (D_MODEL, D_MODEL), dtype=jnp.float32) * scale
        Wo = jax.random.normal(ks[4], (D_MODEL, D_MODEL), dtype=jnp.float32) * scale
        bq = jax.random.normal(ks[5], (D_MODEL,), dtype=jnp.float32) * scale
        bk = jax.random.normal(ks[6], (D_MODEL,), dtype=jnp.float32) * scale
        bv = jax.random.normal(ks[7], (D_MODEL,), dtype=jnp.float32) * scale
        bo = jax.random.normal(ks[8], (D_MODEL,), dtype=jnp.float32) * scale
        return {'x': x, 'Wq': Wq, 'bq': bq, 'Wk': Wk, 'bk': bk, 'Wv': Wv, 'bv': bv, 'Wo': Wo, 'bo': bo}
    _L0_mix_all = _L0_mix_setup()
    _L0_mix_in = {k: v for k, v in _L0_mix_all.items() if k in ('Wq', 'bq', 'Wk', 'bk', 'Wv', 'bv', 'Wo', 'bo')}
    del _L0_mix_all

    def _L0_ffn_setup():
        import jax, jax.numpy as jnp
        import numpy as np
        E = 64
        K = 2
        CAP = 512
        H = 512
        FFN = 256
        B, S = (8, 512)
        key = jax.random.key(seed)
        ks = jax.random.split(key, 6)
        hidden_states = jax.random.normal(ks[0], (B, S, H), dtype=jnp.float32)
        router_w = jax.random.normal(ks[1], (E, H), dtype=jnp.float32) * (0.01 / np.sqrt(H))
        w1 = jax.random.normal(ks[2], (FFN, H), dtype=jnp.float32) * (1.0 / np.sqrt(H))
        b1 = jnp.zeros((FFN,), dtype=jnp.float32)
        w2 = jax.random.normal(ks[3], (H, FFN), dtype=jnp.float32) * (1.0 / np.sqrt(FFN))
        b2 = jnp.zeros((H,), dtype=jnp.float32)
        return {'hidden_states': hidden_states, 'router_w': router_w, 'w1': w1, 'b1': b1, 'w2': w2, 'b2': b2}
    _L0_ffn_all = _L0_ffn_setup()
    _L0_ffn_in = {k: v for k, v in _L0_ffn_all.items() if k in ('router_w', 'w1', 'b1', 'w2', 'b2')}
    del _L0_ffn_all
    return {'x': x, 'src': src, 'dst': dst, 'L0_gnn_W1': _L0_gnn_in['W1'], 'L0_gnn_b1': _L0_gnn_in['b1'], 'L0_gnn_gamma': _L0_gnn_in['gamma'], 'L0_gnn_beta': _L0_gnn_in['beta'], 'L0_gnn_W2': _L0_gnn_in['W2'], 'L0_gnn_b2': _L0_gnn_in['b2'], 'L0_mix_Wq': _L0_mix_in['Wq'], 'L0_mix_bq': _L0_mix_in['bq'], 'L0_mix_Wk': _L0_mix_in['Wk'], 'L0_mix_bk': _L0_mix_in['bk'], 'L0_mix_Wv': _L0_mix_in['Wv'], 'L0_mix_bv': _L0_mix_in['bv'], 'L0_mix_Wo': _L0_mix_in['Wo'], 'L0_mix_bo': _L0_mix_in['bo'], 'L0_ffn_router_w': _L0_ffn_in['router_w'], 'L0_ffn_w1': _L0_ffn_in['w1'], 'L0_ffn_b1': _L0_ffn_in['b1'], 'L0_ffn_w2': _L0_ffn_in['w2'], 'L0_ffn_b2': _L0_ffn_in['b2']}

def reference(x, src, dst, L0_gnn_W1, L0_gnn_b1, L0_gnn_gamma, L0_gnn_beta, L0_gnn_W2, L0_gnn_b2, L0_mix_Wq, L0_mix_bq, L0_mix_Wk, L0_mix_bk, L0_mix_Wv, L0_mix_bv, L0_mix_Wo, L0_mix_bo, L0_ffn_router_w, L0_ffn_w1, L0_ffn_b1, L0_ffn_w2, L0_ffn_b2):
    import jax
    import jax.numpy as jnp

    def _L0_gnn_ref(x, W1, b1, gamma, beta, W2, b2, edge_index):
        import jax, jax.numpy as jnp
        import numpy as np
        N = 1250
        E = 20000
        IN_C = 512
        HID = 512
        OUT_C = 512
        BN_EPS = 1e-05
        n = x.shape[0]
        loops = jnp.arange(n, dtype=edge_index.dtype)
        src = jnp.concatenate([edge_index[0], loops])
        dst = jnp.concatenate([edge_index[1], loops])
        deg = jax.ops.segment_sum(jnp.ones_like(dst, dtype=x.dtype), dst, num_segments=n)
        dinv = jnp.where(deg > 0, deg ** (-0.5), 0.0)
        w = dinv[src] * dinv[dst]

        def agg(h):
            return jax.ops.segment_sum(w[:, None] * h[dst], src, num_segments=n)
        h = x @ W1 + b1
        h = agg(h)
        mu = jnp.mean(h, axis=0)
        var = jnp.var(h, axis=0)
        h = gamma * (h - mu) * jax.lax.rsqrt(var + BN_EPS) + beta
        h = jax.nn.relu(h)
        h = h @ W2 + b2
        h = agg(h)
        return h

    def _L0_mix_ref(x, Wq, bq, Wk, bk, Wv, bv, Wo, bo):
        import jax, jax.numpy as jnp
        import numpy as np
        D_MODEL = 512
        N_HEADS = 8
        D_HEAD = D_MODEL // N_HEADS
        EPS = 1e-06

        def _split_heads(t, B, S):
            return t.reshape(B, S, N_HEADS, D_HEAD).transpose(0, 2, 1, 3)

        def _reference_tuple_inner(x, Wq, bq, Wk, bk, Wv, bv, Wo, bo):
            B, S, _ = x.shape
            q = _split_heads(x @ Wq.T + bq, B, S)
            k = _split_heads(x @ Wk.T + bk, B, S)
            v = _split_heads(x @ Wv.T + bv, B, S)
            q = jax.nn.relu(q)
            k = jax.nn.relu(k)
            k_sum = k.sum(axis=-1, keepdims=True)
            attn = jnp.einsum('bhnd,bhmd->bhnm', q, k) / (k_sum + EPS)
            attn = jax.nn.softmax(attn, axis=-1)
            out = jnp.einsum('bhnm,bhmd->bhnd', attn, v)
            out = out.transpose(0, 2, 1, 3).reshape(B, S, D_MODEL)
            return (out @ Wo.T + bo, attn)
        return _reference_tuple_inner(x, Wq, bq, Wk, bk, Wv, bv, Wo, bo)[0]

    def _L0_ffn_ref(hidden_states, router_w, w1, b1, w2, b2):
        import jax, jax.numpy as jnp
        import numpy as np
        E = 64
        K = 2
        CAP = 512
        H = 512
        FFN = 256
        B, S = (8, 512)
        orig_shape = hidden_states.shape
        x = hidden_states.reshape(-1, orig_shape[-1])
        T = x.shape[0]
        N = T * K
        logits = jnp.einsum('th,eh->te', x, router_w)
        probs_full = jax.nn.softmax(logits, axis=-1)
        probs, idx = jax.lax.top_k(probs_full, K)
        flat_e = idx.reshape(-1)
        flat_p = probs.reshape(-1)
        order = jnp.argsort(flat_e, stable=True)
        sorted_e = flat_e[order]
        counts = jnp.zeros((E,), jnp.int32).at[flat_e].add(1)
        offsets = jnp.concatenate([jnp.zeros((1,), jnp.int32), jnp.cumsum(counts)[:-1]])
        pos = jnp.arange(N, dtype=jnp.int32) - offsets[sorted_e]
        keep = pos < CAP
        slot = sorted_e * CAP + jnp.minimum(pos, CAP - 1)
        dest = jnp.where(keep, slot, E * CAP)
        tok = order // K
        buf = jnp.zeros((E * CAP + 1, x.shape[-1]), x.dtype).at[dest].set(x[tok])
        buf = buf[:-1]
        h = jax.nn.gelu(jnp.einsum('nh,fh->nf', buf, w1) + b1, approximate=False)
        y = jnp.einsum('nf,hf->nh', h, w2) + b2
        gate = jnp.where(keep, flat_p[order], 0.0)
        contrib = y[jnp.minimum(slot, E * CAP - 1)] * gate[:, None]
        out = jnp.zeros_like(x).at[tok].add(contrib)
        return out.reshape(orig_shape)
    edge_index = jnp.stack([src, dst])
    xn = _layernorm(x, axis=-1)
    x = x + _L0_gnn_ref(xn, L0_gnn_W1, L0_gnn_b1, L0_gnn_gamma, L0_gnn_beta, L0_gnn_W2, L0_gnn_b2, edge_index) + _L0_mix_ref(xn[None], L0_mix_Wq, L0_mix_bq, L0_mix_Wk, L0_mix_bk, L0_mix_Wv, L0_mix_bv, L0_mix_Wo, L0_mix_bo)[0]
    x = x + _L0_ffn_ref(_layernorm(x, axis=-1)[None], L0_ffn_router_w, L0_ffn_w1, L0_ffn_b1, L0_ffn_w2, L0_ffn_b2)[0]
    return x

_drawn_inputs = setup_inputs


def setup_inputs(seed=0):
    import zlib

    import numpy as np

    out = dict(_drawn_inputs(seed))
    spreads = {'L0_gnn_b1': (0.0, 0.356),
     'L0_gnn_gamma': (1.0, 0.2),
     'L0_gnn_beta': (0.0, 0.1),
     'L0_gnn_b2': (0.0, 0.1),
     'L0_ffn_b1': (0.0, 0.8),
     'L0_ffn_b2': (0.0, 2.0)}
    factors = {'L0_mix_Wq': 8.0,
     'L0_mix_bq': 37.246,
     'L0_mix_Wk': 8.0,
     'L0_mix_bk': 32.023,
     'L0_mix_Wv': 8.0,
     'L0_mix_bv': 6.994,
     'L0_mix_Wo': 5.914,
     'L0_mix_bo': 3.296,
     'L0_ffn_router_w': 8.0,
     'L0_ffn_w1': 3.323,
     'L0_ffn_w2': 3.03}
    for name, (base, spread) in spreads.items():
        noise = np.random.default_rng([zlib.crc32(name.encode()), seed]).standard_normal(out[name].shape)
        drawn = base * np.exp(spread * noise) if base else spread * noise
        out[name] = jnp.asarray(drawn.astype(out[name].dtype))
    for name, factor in factors.items():
        out[name] = (out[name] * factor).astype(out[name].dtype)
    return out
```

```python
from contextlib import ExitStack

import concourse.bass as bass
from concourse import mybir

F32 = mybir.dt.float32
F32R = mybir.dt.float32r
BF16 = mybir.dt.bfloat16
FP16 = mybir.dt.float16
I32 = mybir.dt.int32
U32 = mybir.dt.uint32
ALU = mybir.AluOpType
ACT = mybir.ActivationFunctionType
AX_X = mybir.AxisListType.X

P = 128
KIB = 1024


class Chain:

    def __init__(self, eng, sem):
        self.eng, self.sem, self.n = eng, sem, 0

    def __call__(self, ins):
        self.n = self.n + 1
        ins.then_inc(self.sem, 1)
        self.eng.wait_ge(self.sem, self.n)


def gps_layer(nc, x, src, dst, W1, b1, gamma, beta, W2, b2, WqT, bq, WkT, bk, WvT, bv, WoT, bo,
              rwT, w1T, fb1, w2T, fb2, out):
    T, D = x.shape
    NB = -(-T // P)
    TP = NB * P
    LAST = T - (NB - 1) * P
    KC = D // P
    H = 8
    DH = D // H
    NPAIR = H // 2
    TILES = [(c, min(512, TP - c)) for c in range(0, TP, 512)]
    KTILES = [(c, min(512, T - c)) for c in range(0, T, 512)]
    NT = len(TILES)
    E = src.shape[0]
    EP = max(p for p in range(1, P + 1) if E % p == 0)
    EC = E // EP
    SC = 4 * P
    NSC = -(-E // SC) + NB
    NSC += NSC % 2
    NCH = 4 * NSC
    NE = rwT.shape[1]
    F = w1T.shape[1]
    FC = F // P
    CAP = 512
    NG = H * NB
    EPS_K, EPS_LN = 1e-6, 1e-5

    q_dram = nc.dram_tensor("q_scratch", [2, D, TP], F32, kind="Internal").ap()
    k_dram = nc.dram_tensor("k_scratch", [2, D, TP], F32, kind="Internal").ap()
    v_dram = nc.dram_tensor("v_scratch", [P, H, NB * P], F32, kind="Internal").ap()
    e_dram = nc.dram_tensor("edge_scratch", [P * NCH, 2], I32, kind="Internal").ap()

    with ExitStack() as ctx:
        def sb(name, shape, dt):
            return ctx.enter_context(nc.sbuf_tensor(name, shape, dt))

        def sem(name):
            return ctx.enter_context(nc.semaphore(name))

        ident = sb("ident", [P, P], F32)
        mask_a = sb("mask_a", [P, P], F32)
        mask_b = sb("mask_b", [P, P], F32)
        head_ones = sb("head_ones", [P, P], F32)
        before = sb("before", [P, P], F32)
        iota_f = sb("iota_f", [P, P], F32)
        iota_h = sb("iota_h", [P, TP], FP16)
        ln_mv = sb("ln_mv", [P, NB, 2], F32)
        ln_st = sb("ln_st", [P, NB, 6], F32)
        rstd = sb("rstd", [P, NB], F32)
        nt_a = sb("nt_a", [P, NB], F32)
        nt_i = sb("nt_i", [P, NB], I32)
        rowsum = sb("rowsum", [P, NG], F32)
        negr = sb("negr", [P, NG], F32)
        negmax = sb("negmax", [P, 2], F32)
        dinv = sb("dinv", [P, NB], F32)
        deg = sb("deg", [P, NB], F32)
        var_c = sb("var_c", [P, NB], F32)
        bq_sb = sb("bq_sb", [P, KC], F32)
        bk_sb = sb("bk_sb", [P, KC], F32)
        gamma_sb = sb("gamma_sb", [P, KC], F32)
        beta_sb = sb("beta_sb", [P, KC], F32)
        fb1_sb = sb("fb1_sb", [P, FC], F32)
        pos_i = sb("pos_i", [EP, EC], I32)
        pairs = sb("pairs", [EP, EC, 2], I32)
        bkt_row = sb("bkt_row", [1, NSC], I32)
        small = sb("small", [P, 2 * KC], F32)
        top8 = sb("top8", [P, NB, 8], F32)
        idx8 = sb("idx8", [P, NB, 8], U32)

        arena_base = -(-nc.sbuf_base // 64) * 64

        def at(name, kib, shape, dt):
            return nc.alloc_sbuf_tensor_at(name, shape, dt, offset=arena_base + int(kib * KIB))

        H1 = at("H1", 177, [P, NB, D], F32)
        VV = at("VV", 0, [P, H, NB, P], F32R)
        XT = [at("xt_hi", 40, [P, KC, TP], F32R), at("xt_lo", 60, [P, KC, TP], F32R)]
        WH = [[at(f"w{r}_{'hl'[k]}", 80 + 16 * r + 8 * k, [P, KC, D], F32R) for k in range(2)] for r in range(2)]
        WRAW = [at(f"wraw{r}", 112 + 8 * r, [P, KC, D], F32) for r in range(2)]
        X = at("X", 128, [P, NB, D], F32)
        QF = [at(f"qf{r}", 128 + 15 * r, [P, TP], F32) for r in range(2)]
        QH = [at(f"qh{r}", 133 + 15 * r, [P, TP], F32R) for r in range(2)]
        QL = [at(f"ql{r}", 138 + 15 * r, [P, TP], F32R) for r in range(2)]
        bv_all = at("bv_all", 158, [P, D], F32)
        b1_all = at("b1_all", 160, [P, D], F32)
        vt = at("vt", 162, [P, 2, D], F32)
        ones_c = at("ones_c", 166, [P, 512], F32)
        e_src = at("e_src", 168, [EP, EC], I32)
        e_dst = at("e_dst", 168.75, [EP, EC], I32)
        e_bkt = at("e_bkt", 169.5, [EP, EC], I32)
        e_bf = at("e_bf", 170.25, [EP, EC], F32)
        e_mask = at("e_mask", 171, [EP, EC], F32)
        e_cum = at("e_cum", 171.75, [EP, EC], F32)
        e_pos = at("e_pos", 172.5, [EP, EC], F32)
        e_tmp = at("e_tmp", 173.25, [EP, EC], I32)
        e_tot = at("e_tot", 174, [P, NB], F32)
        e_base = at("e_base", 174.125, [P, NB], F32)
        e_cnt = at("e_cnt", 174.25, [P, NB], F32)
        e_cnti = at("e_cnti", 174.375, [P, NB], I32)
        e_end = at("e_end", 174.5, [P, NB], F32)
        e_nsc = at("e_nsc", 174.625, [P, NB], F32)
        e_acc = at("e_acc", 174.75, [1, NSC], F32)
        e_fill = at("e_fill", 175, [P, NCH * 2 // 4], I32)
        QS = [at(f"qs{r}", 0 + 20 * r, [P, 2, TP], F32R) for r in range(2)]
        KS = [at(f"ks{r}", 10 + 20 * r, [P, TP], F32R) for r in range(2)]
        VS = [at(f"vs{r}", 15 + 20 * r, [P, NB, P], F32R) for r in range(2)]
        PT = [[at(f"pt{r}{'hl'[k]}", 40 + 20 * r + 10 * k, [P, NB, 2 * P], F32R) for k in range(2)] for r in range(2)]
        SN = [at(f"sn{r}", 80 + 5 * r, [P, T], F32) for r in range(2)]
        PR = [at(f"pr{r}", 90 + 5 * r, [P, TP], F32) for r in range(2)]
        OP = at("OP", 100, [P, NPAIR, TP], F32)
        OM = at("OM", 120, [P, NPAIR, TP], F32)
        DG = [at(f"dg{r}", 80 + 5 * r, [P, NB, P], F32) for r in range(2)]
        ON = [at("on_hi", 40, [P, NPAIR, TP], F32R), at("on_lo", 60, [P, NPAIR, TP], F32R)]
        WO = [at("wo_hi", 0, [P, KC, D], F32R), at("wo_lo", 8, [P, KC, D], F32R)]
        WO_RAW = at("wo_raw", 140, [P, KC, D], F32)
        XR = at("XR", 16, [P, NB, D], F32)
        bo_all = at("bo_all", 36, [P, D], F32)
        ACC = at("ACC", 157, [P, NB, D], F32)
        CT = at("CT", 105, [P, NB, TP], F32)
        CTR = at("CTR", 105, [P, NB, TP], F32R)
        OHS = [at(f"ohs{r}", 80 + 2.5 * r, [P, TP], BF16) for r in range(8)]
        OHD = [at(f"ohd{r}", 100 + 0.25 * r, [P, P], BF16) for r in range(8)]
        e_load = at("e_load", 102, [P, NCH, 2], I32)
        e_df = at("e_df", 103.625, [P, NCH], F32)
        e_sf = at("e_sf", 36, [P, NCH], F32)
        DGD = at("DGD", 16, [P, NB, P], F32)
        HS = [at("hs_hi", 60, [P, NB, D], F32R), at("hs_lo", 80, [P, NB, D], F32R)]
        G = at("G", 16, [P, KC, TP], F32)
        dinv_all = at("dinv_all", 36, [P, TP], F32)
        GR = [at("gr_hi", 60, [P, KC, TP], F32R), at("gr_lo", 80, [P, KC, TP], F32R)]
        W2H = [at("w2_hi", 0, [P, KC, D], F32R), at("w2_lo", 8, [P, KC, D], F32R)]
        W2_RAW = at("w2_raw", 42, [P, KC, D], F32)
        b2_all = at("b2_all", 50, [P, D], F32)
        ht = at("ht", 52, [P, 2, D], F32)
        H2 = [at("h2_hi", 16, [P, NB, D], F32R), at("h2_lo", 177, [P, NB, D], F32R)]
        XN = at("XN", 40, [P, NB, D], F32)
        X2T = [at("x2t_hi", 60, [P, KC, TP], F32R), at("x2t_lo", 80, [P, KC, TP], F32R)]
        RW_RAW = at("rw_raw", 0, [P, KC, NE], F32)
        RW = [at("rw_hi", 1, [P, KC, NE], F32R), at("rw_lo", 2, [P, KC, NE], F32R)]
        F1_RAW = at("f1_raw", 3, [P, KC, F], F32)
        F1 = [at("f1_hi", 7, [P, KC, F], F32R), at("f1_lo", 11, [P, KC, F], F32R)]
        F2_RAW = at("f2_raw", 15, [P, FC, D], F32)
        F2 = [at("f2_hi", 19, [P, FC, D], F32R), at("f2_lo", 23, [P, FC, D], F32R)]
        fb2_all = at("fb2_all", 27, [P, D], F32)
        LG = at("LG", 29, [P, NB, NE], F32)
        EL = at("EL", 31.5, [P, NB, NE], F32)
        MK = at("MK", 34, [P, NB, NE], F32)
        MR = at("MR", 36.5, [P, NB, NE], F32)
        gate = at("gate", 39, [P, NB], F32)
        zsum = at("zsum", 39.125, [P, NB], F32)
        l1neg = at("l1neg", 39.25, [P, NB], F32)
        idxf = at("idxf", 39.5, [P, NB, 8], F32)
        HF = at("HF", 105, [P, FC, TP], F32)
        HFH = [at("hf_hi", 115, [P, FC, TP], F32R), at("hf_lo", 125, [P, FC, TP], F32R)]
        yt = at("yt", 135, [P, D], F32)

        PS = ctx.enter_context(nc.psum_tensor("PS", [P, 8, 512], F32))
        ps_flat = PS[:, :, :].rearrange("p a b -> p (a b)")

        const_done = sem("const_done")
        x_pad = sem("x_pad")
        x_in = [sem(f"x_in{b}") for b in range(NB)]
        bias_in = sem("bias_in")
        edge_in = sem("edge_in")
        w_in = [sem(f"w_in{n}") for n in range(4)]
        w_hi = sem("w_hi")
        w_lo = sem("w_lo")
        dve = sem("dve_step")
        acts = sem("act_step")
        pool = sem("pool_step")
        pes = sem("pe_step")
        fill_set = sem("fill_set")
        fill_out = sem("fill_out")
        etot_ready = sem("etot_ready")
        epre_ready = sem("epre_ready")
        scat_ready = sem("scat_ready")
        scat_done = sem("scat_done")
        edges_back = sem("edges_back")
        xn_ready = sem("xn_ready")
        xt_ps = sem("xt_ps")
        xt_hi = sem("xt_hi")
        xt_lo = sem("xt_lo")
        v_ps = sem("v_ps")
        v_biased = sem("v_biased")
        v_hi = sem("v_hi")
        v_lo = sem("v_lo")
        v_out = sem("v_out")
        h1_ps = sem("h1_ps")
        h1_done = sem("h1_done")
        qk_ps = sem("qk_ps")
        qk_relu = sem("qk_relu")
        qk_act = sem("qk_act")
        qk_lo = sem("qk_lo")
        ks_ps = sem("ks_ps")
        ks_read = sem("ks_read")
        qk_out = [sem("qk_out0"), sem("qk_out1")]
        stack_in = [sem("stack_in0"), sem("stack_in1")]
        s_ready = sem("s_ready")
        s_neg = sem("s_neg")
        p_exp = sem("p_exp")
        p_pad = sem("p_pad")
        pt_ps = sem("pt_ps")
        pt_hi = sem("pt_hi")
        pt_lo = sem("pt_lo")
        av_done = sem("av_done")
        o_out = sem("o_out")
        rinv_done = sem("rinv_done")
        diag_done = sem("diag_done")
        o_sum = sem("o_sum")
        r_ps = sem("r_ps")
        on_f = sem("on_f")
        on_hi = sem("on_hi")
        on_lo = sem("on_lo")
        wo_in = sem("wo_in")
        wo_hi = sem("wo_hi")
        wo_lo = sem("wo_lo")
        xr_in = sem("xr_in")
        xr_b = sem("xr_b")
        wo_ps = sem("wo_ps")
        acc_done = sem("acc_done")
        oh_ready = sem("oh_ready")
        oh_used = sem("oh_used")
        ct_ps = sem("ct_ps")
        ct_add = sem("ct_add")
        ct_ready = sem("ct_ready")
        dd_ready = sem("dd_ready")
        dr_ps = sem("dr_ps")
        dr_done = sem("dr_done")
        h1_scaled = sem("h1_scaled")
        hs_hi = sem("hs_hi")
        hs_lo = sem("hs_lo")
        g_ps = sem("g_ps")
        g_done = sem("g_done")
        bn_done = sem("bn_done")
        gr_relu = sem("gr_relu")
        gr_hi = sem("gr_hi")
        gr_lo = sem("gr_lo")
        w2_in = sem("w2_in")
        w2_hi = sem("w2_hi")
        w2_lo = sem("w2_lo")
        h2_ps = sem("h2_ps")
        h2_b = sem("h2_b")
        h2_hi = sem("h2_hi")
        h2_lo = sem("h2_lo")
        a2_ps = sem("a2_ps")
        x2_done = sem("x2_done")
        xn2_ready = sem("xn2_ready")
        x2t_ps = sem("x2t_ps")
        x2t_hi = sem("x2t_hi")
        x2t_lo = sem("x2t_lo")
        f_in = sem("f_in")
        f_hi = sem("f_hi")
        f_lo = sem("f_lo")
        lg_ps = sem("lg_ps")
        lg_done = sem("lg_done")
        top_done = sem("top_done")
        el_done = sem("el_done")
        mk_done = sem("mk_done")
        ps_pos = sem("ps_pos")
        u_ps = sem("u_ps")
        u_gelu = sem("u_gelu")
        u_hi = sem("u_hi")
        u_lo = sem("u_lo")
        y_ps = sem("y_ps")
        gate_done = sem("gate_done")
        y_b = sem("y_b")
        y_done = sem("y_done")
        out_done = sem("out_done")

        block = ctx.enter_context(nc.Block())

        def blk(b):
            return slice(b * P, (b + 1) * P)

        PARTS = [(0, 4), (4, NB)]

        def pt_banks(b0, b1):
            return ps_flat[:, 3 * 512 + b0 * P:3 * 512 + b1 * P].rearrange("p (b t) -> p b t", b=b1 - b0)

        def row_bcast(v):
            return v.rearrange("(a n) -> a n", a=1).to_broadcast([P, v.shape[0]])

        def w_view(w):
            return w.rearrange("(c p) n -> p c n", p=P)

        @block.sync
        def _(sp):
            sp.dma_start(e_dst[:, :], dst.rearrange("(p c) -> p c", p=EP)).then_inc(edge_in, 16)
            sp.dma_start(e_src[:, :], src.rearrange("(p c) -> p c", p=EP)).then_inc(edge_in, 16)
            for b in range(NB - 1):
                sp.dma_start(X[:, b, :], x[blk(b), :]).then_inc(x_in[b], 16)
            sp.wait_ge(x_pad, 1)
            sp.dma_start(X[0:LAST, NB - 1, :], x[(NB - 1) * P:T, :]).then_inc(x_in[NB - 1], 16)
            sp.dma_start(WRAW[0][:, :, :], w_view(WvT)).then_inc(w_in[0], 16)
            sp.dma_start(WRAW[1][:, :, :], w_view(W1)).then_inc(w_in[1], 16)
            sp.dma_start(bv_all[:, :], row_bcast(bv)).then_inc(bias_in, 16)
            sp.dma_start(b1_all[:, :], row_bcast(b1)).then_inc(bias_in, 16)
            with nc.allow_non_contiguous_dma(reason="biases, one element per partition"):
                for tile, vec in ((bq_sb, bq), (bk_sb, bk), (gamma_sb, gamma), (beta_sb, beta), (fb1_sb, fb1)):
                    sp.dma_start(tile[:, :], vec.rearrange("(c p) -> p c", p=P)).then_inc(bias_in, 16)
            sp.wait_ge(fill_set, 1)
            for r in range(4):
                sp.dma_start(e_dram.rearrange("(p c) t -> p (c t)", p=P)[:, r * (NCH // 2):(r + 1) * (NCH // 2)],
                             e_fill[:, :]).then_inc(fill_out, 16)
            for r, w in enumerate((WqT, WkT)):
                sp.wait_ge(w_lo, r + 1)
                sp.dma_start(WRAW[r][:, :, :], w_view(w)).then_inc(w_in[2 + r], 16)
            sp.wait_ge(v_lo, NB)
            sp.dma_start(v_dram, VV[:, :, :, :].bitcast(F32).rearrange("p h b d -> p h (b d)")).then_inc(v_out, 16)
            for j in range(2 * NPAIR):
                sp.wait_ge(qk_lo, NT * (j + 1))
                pr, d = j % NPAIR, (q_dram if j < NPAIR else k_dram)
                sp.dma_start(d[0, blk(pr), :], QH[j % 2][:, :].bitcast(F32)).then_inc(qk_out[j % 2], 16)
                sp.dma_start(d[1, blk(pr), :], QL[j % 2][:, :].bitcast(F32)).then_inc(qk_out[j % 2], 16)
            sp.wait_ge(v_out, 16)
            sp.wait_ge(qk_out[0], 32 * NPAIR)
            sp.wait_ge(qk_out[1], 32 * NPAIR)
            sp.wait_ge(h1_done, NB)

            def load_head(h, slot):
                rows = bass.ds(h * DH, DH)
                for half in range(2):
                    part = slice(half * DH, (half + 1) * DH)
                    sp.dma_start(QS[slot][part, :, :].bitcast(F32),
                                 q_dram[:, rows, :].rearrange("l d t -> d l t")).then_inc(stack_in[slot], 16)
                    sp.dma_start(KS[slot][part, :].bitcast(F32), k_dram[half, rows, :]).then_inc(stack_in[slot], 16)
                sp.dma_start(VS[slot][:, :, :].bitcast(F32).rearrange("p b d -> p (b d)"),
                             v_dram[:, bass.ds(h, 1), :].rearrange("p a n -> p (a n)")).then_inc(stack_in[slot], 16)

            load_head(0, 0)
            load_head(1, 1)
            with sp.Fori(1, NPAIR) as p:
                for s in range(2):
                    sp.wait_ge(av_done, (p - 1) * NB + (s + 1) * (NB // 2))
                    load_head(p * 2 + s, s)
            sp.wait_ge(av_done, NG // 2)
            sp.dma_start(WO_RAW[:, :, :], w_view(WoT)).then_inc(wo_in, 16)
            sp.wait_ge(x_pad, 2)
            sp.dma_start(XR[:, 0:NB - 1, :], x[0:(NB - 1) * P, :].rearrange("(b p) d -> p b d", p=P)).then_inc(xr_in, 16)
            sp.dma_start(XR[0:LAST, NB - 1, :], x[(NB - 1) * P:T, :]).then_inc(xr_in, 16)
            sp.dma_start(bo_all[:, :], row_bcast(bo)).then_inc(xr_in, 16)
            sp.wait_ge(on_lo, NPAIR * NT)
            sp.wait_ge(scat_done, 16 * EC)
            sp.dma_start(e_load[:, :, :].rearrange("p c t -> p (c t)"),
                         e_dram.rearrange("(p c) t -> p (c t)", p=P)).then_inc(edges_back, 16)
            DGD = at("DGD", 16, [P, NB, P], F32)
            sp.wait_ge(acc_done, NB)
            sp.dma_start(W2_RAW[:, :, :], w_view(W2)).then_inc(w2_in, 16)
            sp.dma_start(b2_all[:, :], row_bcast(b2)).then_inc(w2_in, 16)
            sp.wait_ge(x2_done, NB)
            sp.dma_start(RW_RAW[:, :, :], w_view(rwT)).then_inc(f_in, 16)
            sp.dma_start(F1_RAW[:, :, :], w_view(w1T)).then_inc(f_in, 16)
            sp.dma_start(F2_RAW[:, :, :], w_view(w2T)).then_inc(f_in, 16)
            sp.dma_start(fb2_all[:, :], row_bcast(fb2)).then_inc(f_in, 16)
            for b in range(NB):
                n = P if b < NB - 1 else LAST
                sp.wait_ge(y_done, b + 1)
                sp.dma_start(out[b * P:b * P + n, :], ACC[0:n, b, :]).then_inc(out_done, 16)
            sp.wait_ge(out_done, 16 * NB)

        @block.gpsimd
        def _(gp):
            link = Chain(gp, pool)
            nc.gpsimd.memset(X[:, NB - 1, :], 0.0).then_inc(x_pad, 1)
            nc.gpsimd.memset(e_fill[:, :], -1).then_inc(fill_set, 1)
            nc.gpsimd.memset(ones_c[:, :], 1.0)
            nc.gpsimd.memset(mask_a[:, 0:DH], 1.0)
            nc.gpsimd.memset(mask_a[:, DH:P], 0.0)
            nc.gpsimd.memset(mask_b[:, 0:DH], 0.0)
            nc.gpsimd.memset(mask_b[:, DH:P], 1.0)
            link(nc.gpsimd.memset(head_ones[:, :], 0.0))
            link(nc.gpsimd.memset(head_ones[0:DH, 0:DH], 1.0))
            link(nc.gpsimd.memset(head_ones[DH:P, DH:P], 1.0))
            nc.gpsimd.memset(ident[:, :], 0.0)
            link(nc.gpsimd.memset(before[:, :], 1.0))
            nc.gpsimd.affine_select(out=ident[:, :], in_=ident[:, :], compare_op=ALU.not_equal, fill=1.0,
                                    base=0, pattern=[[-1, P]], channel_multiplier=1)
            nc.gpsimd.affine_select(out=before[:, :], in_=before[:, :], compare_op=ALU.is_gt, fill=0.0,
                                    base=0, pattern=[[1, P]], channel_multiplier=-1)
            nc.gpsimd.iota(iota_f[:, :], pattern=[[1, P]], base=0, channel_multiplier=0,
                           allow_small_or_imprecise_dtypes=True)
            nc.gpsimd.iota(iota_h[:, :], pattern=[[1, TP]], base=0, channel_multiplier=0,
                           allow_small_or_imprecise_dtypes=True).then_inc(const_done, 1)
            gp.wait_ge(fill_out, 64)
            gp.wait_ge(scat_ready, 1)
            for c in range(EC):
                nc.gpsimd.indirect_dma_start(
                    out=e_dram, out_offset=bass.IndirectOffsetOnAxis(ap=pos_i[:, c:c + 1], axis=0),
                    in_=pairs[:, c, :], in_offset=None).then_inc(scat_done, 16)
            gp.wait_ge(av_done, NG // 2)
            nc.gpsimd.memset(XR[:, NB - 1, :], 0.0).then_inc(x_pad, 1)
            gp.wait_ge(rinv_done, 1)
            for p in range(NPAIR):
                gp.wait_ge(r_ps, p * NT)
                for s in range(2):
                    nc.gpsimd.tensor_tensor(
                        DG[s][:, :, :], ident[:, None, :].to_broadcast([P, NB, P]),
                        rowsum[:, p * (2 * NB) + s * NB:p * (2 * NB) + (s + 1) * NB].rearrange("p (a b) -> p a b", b=1).to_broadcast([P, NB, P]),
                        ALU.mult).then_inc(diag_done, 1)
            gp.wait_ge(xr_in, 48)
            nc.gpsimd.tensor_tensor(XR[:, :, :], XR[:, :, :], bo_all[:, None, :].to_broadcast([P, NB, D]),
                                    ALU.add).then_inc(xr_b, 1)
            gp.wait_ge(dd_ready, 1)
            nc.gpsimd.tensor_tensor(DGD[:, :, :], ident[:, None, :].to_broadcast([P, NB, P]),
                                    dinv[:, :, None].to_broadcast([P, NB, P]), ALU.mult).then_inc(diag_done, 1)

        def one(ap3):
            return ap3.rearrange("p a d -> p (a d)")

        @block.scalar
        def _(act):
            def xt_high(b):
                act.wait_ge(xt_ps, b + 1)
                nc.scalar.activation(XT[0][:, :, bass.ds(b * P, P)],
                                     PS[:, bass.ds(b % 2, 1), :].rearrange("p a (c t) -> p (a c) t", c=KC),
                                     ACT.Copy).then_inc(xt_hi, 1)

            def v_high(b):
                act.wait_ge(v_biased, b + 1)
                nc.scalar.activation(VV[:, :, bass.ds(b, 1), 0:DH].rearrange("p h a d -> p (h a) d"),
                                     vt[:, bass.ds(b % 2, 1), :].rearrange("p a (h d) -> p (a h) d", h=H),
                                     ACT.Copy).then_inc(v_hi, 1)

            xt_high(0)
            xt_high(1)
            for n in range(2):
                act.wait_ge(w_in[n], 16)
                nc.scalar.activation(WH[n][0][:, :, :], WRAW[n][:, :, :], ACT.Copy).then_inc(w_hi, 1)
            with act.Fori(0, NB - 2) as b:
                v_high(b)
                xt_high(b + 2)
            v_high(NB - 2)
            v_high(NB - 1)
            for n in range(2):
                act.wait_ge(w_in[n + 2], 16)
                act.wait_ge((v_ps, h1_ps)[n], NB)
                nc.scalar.activation(WH[n][0][:, :, :], WRAW[n][:, :, :], ACT.Copy).then_inc(w_hi, 1)
            act.wait_ge(bias_in, 16 * 7)
            act.wait_ge(xn_ready, NB)
            act.wait_ge(xt_ps, NB)
            for j in range(2 * NPAIR):
                pr = j % NPAIR
                bias = (bq_sb if j < NPAIR else bk_sb)[:, pr:pr + 1]
                if j >= 2:
                    act.wait_ge(qk_out[j % 2], 32 * (j // 2))
                if j >= NPAIR + 2:
                    act.wait_ge(ks_read, j - NPAIR - 1)
                for t, (c0, w) in enumerate(TILES):
                    n = NT * j + t
                    act.wait_ge(qk_ps, n + 1)
                    nc.scalar.activation(QF[j % 2][:, c0:c0 + w], PS[:, n % 4, 0:w], ACT.Relu, bias=bias)
                    nc.scalar.activation(QH[j % 2][:, c0:c0 + w], PS[:, n % 4, 0:w], ACT.Relu,
                                         bias=bias).then_inc(qk_act, 1)

            def exp_step(p, i):
                g = p * (2 * NB) + i
                act.wait_ge(s_neg, g + 1)
                if not (first(p) and i < 2):
                    act.wait_ge(pt_ps, g * 2 - 2)
                nc.scalar.activation(PR[i % 2][:, 0:T], SN[i % 2][:, :], ACT.Exp, scale=-1.0,
                                     bias=negmax[:, i % 2:i % 2 + 1],
                                     accum_out=rowsum[:, bass.ds(g, 1)]).then_inc(p_exp, 1)

            def hi_step(p, i):
                g = p * (2 * NB) + i
                if i % 2 == 0 and not (first(p) and i < 4):
                    act.wait_ge(av_done, p * NB + i // 2 - 1)
                for part, (b0, b1) in enumerate(PARTS):
                    act.wait_ge(pt_ps, g * 2 + (part + 1))
                    nc.scalar.activation(PT[i // 2 % 2][0][:, b0:b1, (i % 2) * P:(i % 2 + 1) * P], pt_banks(b0, b1),
                                         ACT.Copy).then_inc(pt_hi, 1)

            def out_step(p, k):
                a, m = ((OP, OM) if k < NB // 2 else (OM, OP))
                cols = slice((k % (NB // 2)) * 2 * P, (k % (NB // 2) + 1) * 2 * P)
                act.wait_ge(av_done, p * NB + k + 1)
                keep, move = ((slice(0, DH), slice(DH, P)) if k < NB // 2 else (slice(DH, P), slice(0, DH)))
                nc.scalar.activation(one(OP[keep, bass.ds(p, 1), cols]), PS[keep, 6 + k % 2, 0:2 * P], ACT.Copy)
                nc.scalar.activation(one(OM[keep, bass.ds(p, 1), cols]), PS[move, 6 + k % 2, 0:2 * P],
                                     ACT.Copy).then_inc(o_out, 1)

            def first(p):
                return type(p) is int and p == 0

            def att_steps(p):
                for i in range(2 * NB):
                    if i > 0:
                        hi_step(p, i - 1)
                    elif not first(p):
                        hi_step(p - 1, 2 * NB - 1)
                    exp_step(p, i)
                    if i % 2 == 1:
                        k = (i - 5) // 2
                        if k >= 0:
                            out_step(p, k)
                        elif not first(p):
                            out_step(p - 1, k + NB)

            att_steps(0)
            with act.Fori(1, NPAIR) as p:
                att_steps(p)
            hi_step(NPAIR - 1, 2 * NB - 1)
            for k in range(NB - 2, NB):
                out_step(NPAIR - 1, k)

            act.wait_ge(wo_in, 16)
            nc.scalar.activation(WO[0][:, :, :], WO_RAW[:, :, :], ACT.Copy).then_inc(wo_hi, 1)
            for p in range(NPAIR):
                for t, (c0, w) in enumerate(TILES):
                    act.wait_ge(on_f, NT * p + t + 1)
                    nc.scalar.activation(ON[0][:, p, c0:c0 + w], OP[:, p, c0:c0 + w], ACT.Copy).then_inc(on_hi, 1)

            act.wait_ge(w2_in, 32)
            nc.scalar.activation(W2H[0][:, :, :], W2_RAW[:, :, :], ACT.Copy).then_inc(w2_hi, 1)
            for t, (c0, w) in enumerate(TILES):
                act.wait_ge(dr_ps, t + 1)
                nc.scalar.activation(dinv_all[:, c0:c0 + w], PS[:, t, 0:w], ACT.Copy).then_inc(dr_done, 1)
            with act.Fori(0, NB) as b:
                act.wait_ge(h1_scaled, b + 1)
                nc.scalar.activation(HS[0][:, bass.ds(b, 1), :], H1[:, bass.ds(b, 1), :], ACT.Copy).then_inc(hs_hi, 1)
            act.wait_ge(g_ps, KC * NT)
            for c in range(KC):
                act.wait_ge(bn_done, 1)
                nc.scalar.activation(G[:, c, :], G[:, c, :], ACT.Relu, scale=small[:, c:c + 1],
                                     bias=small[:, KC + c:KC + c + 1]).then_inc(gr_relu, 1)
                act.wait_ge(gr_relu, c + 1)
                nc.scalar.activation(GR[0][:, c, :], G[:, c, :], ACT.Copy).then_inc(gr_hi, 1)
            act.wait_ge(gr_lo, KC)
            with act.Fori(0, NB) as b:
                act.wait_ge(h2_b, b + 1)
                nc.scalar.activation(one(H2[0][:, bass.ds(b, 1), :]), one(ht[:, bass.ds(b % 2, 1), :]), ACT.Copy,
                                     scale=dinv[:, bass.ds(b, 1)]).then_inc(h2_hi, 1)

            act.wait_ge(f_in, 64)
            for raw, hi in ((RW_RAW, RW[0]), (F1_RAW, F1[0]), (F2_RAW, F2[0])):
                nc.scalar.activation(hi[:, :, :], raw[:, :, :], ACT.Copy).then_inc(f_hi, 1)
            with act.Fori(0, NB) as b:
                act.wait_ge(x2t_ps, b + 1)
                nc.scalar.activation(X2T[0][:, :, bass.ds(b * P, P)],
                                     PS[:, bass.ds(b % 4, 1), :].rearrange("p a (c t) -> p (a c) t", c=KC),
                                     ACT.Copy).then_inc(x2t_hi, 1)
            act.wait_ge(top_done, 1)
            with act.Fori(0, NB) as b:
                nc.scalar.activation(one(EL[:, bass.ds(b, 1), :]), one(LG[:, bass.ds(b, 1), :]), ACT.Exp,
                                     bias=l1neg[:, bass.ds(b, 1)], accum_out=zsum[:, bass.ds(b, 1)]).then_inc(el_done, 1)
            for f in range(FC):
                for t, (c0, w) in enumerate(TILES):
                    n = NT * f + t
                    act.wait_ge(u_ps, n + 1)
                    nc.scalar.activation(HF[:, f, c0:c0 + w], PS[:, n % 4, 0:w], ACT.Gelu,
                                         bias=fb1_sb[:, f:f + 1]).then_inc(u_gelu, 1)
                    act.wait_ge(u_gelu, n + 1)
                    nc.scalar.activation(HFH[0][:, f, c0:c0 + w], HF[:, f, c0:c0 + w], ACT.Copy).then_inc(u_hi, 1)

        @block.vector
        def _(ve):
            V = nc.vector
            link = Chain(ve, dve)

            def rsqrt(out_t, in_t, n):
                t, ti = nt_a[:, 0:n], nt_i[:, 0:n]
                link(V.tensor_scalar(ti, in_t.bitcast(I32), 1, None, ALU.logical_shift_right))
                link(V.tensor_scalar(out_t.bitcast(I32), ti, float(-0x5F3759DF), -1.0, ALU.add, ALU.mult))
                for _ in range(3):
                    link(V.scalar_tensor_tensor(t, out_t, -0.5, out_t, ALU.mult, ALU.mult))
                    link(V.tensor_tensor(t, t, in_t, ALU.mult))
                    link(V.scalar_tensor_tensor(out_t, t, 1.5, out_t, ALU.add, ALU.mult))

            def layernorm(src_t, dst_t, arrived, done, groups):
                for b0, b1 in groups:
                    for b in range(b0, b1):
                        arrived(b)
                        last = V.bn_stats(ln_st[:, b, :], src_t[:, b, :])
                    link(last)
                    for b in range(b0, b1):
                        last = V.bn_aggr(ln_mv[:, b, :], ln_st[:, b, :])
                    link(last)
                    link(V.tensor_scalar(var_c[:, b0:b1], ln_mv[:, b0:b1, 1], EPS_LN, None, ALU.add))
                    rsqrt(rstd[:, b0:b1], var_c[:, b0:b1], b1 - b0)
                    for b in range(b0, b1):
                        V.tensor_scalar(dst_t[:, b, :], src_t[:, b, :], ln_mv[:, b, 0:1], rstd[:, b:b + 1],
                                        ALU.subtract, ALU.mult).then_inc(done, 1)

            ve.wait_ge(edge_in, 32)
            ve.wait_ge(const_done, 1)
            link(V.tensor_scalar(e_bkt[:, :], e_dst[:, :], 7, None, ALU.logical_shift_right))
            link(V.tensor_copy(e_bf[:, :], e_bkt[:, :]))

            def bucket_total(b):
                V.tensor_scalar(e_mask[:, :], e_bf[:, :], iota_f[0:EP, bass.ds(b, 1)], None, ALU.is_equal, ALU.add,
                                accum_out=e_tot[0:EP, bass.ds(b, 1)]).then_inc(etot_ready, 1)

            bucket_total(0)
            with ve.Fori(1, NB) as b:
                ve.wait_ge(etot_ready, b)
                bucket_total(b)

            layernorm(X, X, lambda b: ve.wait_ge(x_in[b], 16), xn_ready, [(0, 2), (2, 6), (6, NB)])

            def weight_low(n):
                ve.wait_ge(w_hi, n + 1)
                V.tensor_tensor(WH[n % 2][1][:, :, :], WRAW[n % 2][:, :, :], WH[n % 2][0][:, :, :].bitcast(F32),
                                ALU.subtract).then_inc(w_lo, 1)

            def xt_low(b):
                ve.wait_ge(xt_hi, b + 1)
                V.tensor_tensor(XT[1][:, :, bass.ds(b * P, P)],
                                PS[:, bass.ds(b % 2, 1), :].rearrange("p a (c t) -> p (a c) t", c=KC),
                                XT[0][:, :, bass.ds(b * P, P)].bitcast(F32), ALU.subtract).then_inc(xt_lo, 1)

            def v_bias(b):
                ve.wait_ge(v_ps, b + 1)
                V.tensor_tensor(one(vt[:, bass.ds(b % 2, 1), :]), one(PS[:, bass.ds(b % 2 + 2, 1), :]), bv_all[:, :],
                                ALU.add).then_inc(v_biased, 1)

            def h1_bias(b):
                ve.wait_ge(h1_ps, b + 1)
                V.tensor_tensor(one(H1[:, bass.ds(b, 1), :]), one(PS[:, bass.ds(b % 2 + 4, 1), :]), b1_all[:, :],
                                ALU.add).then_inc(h1_done, 1)

            def v_low(b):
                ve.wait_ge(v_hi, b + 1)
                V.tensor_tensor(VV[:, :, bass.ds(b, 1), DH:P].rearrange("p h a d -> p (h a) d"),
                                vt[:, bass.ds(b % 2, 1), :].rearrange("p a (h d) -> p (a h) d", h=H),
                                VV[:, :, bass.ds(b, 1), 0:DH].rearrange("p h a d -> p (h a) d").bitcast(F32),
                                ALU.subtract).then_inc(v_lo, 1)

            xt_low(0)
            xt_low(1)
            weight_low(0)
            weight_low(1)
            ve.wait_ge(bias_in, 16 * 7)
            for b in range(2):
                v_bias(b)
                h1_bias(b)
                v_low(b)
                xt_low(b + 2)
            with ve.Fori(2, NB - 2) as b:
                ve.wait_ge(v_lo, b - 1)
                v_bias(b)
                h1_bias(b)
                v_low(b)
                xt_low(b + 2)
            ve.wait_ge(v_lo, NB - 3)
            v_bias(NB - 2)
            h1_bias(NB - 2)
            v_low(NB - 2)
            ve.wait_ge(v_lo, NB - 2)
            v_bias(NB - 1)
            weight_low(2)
            h1_bias(NB - 1)
            v_low(NB - 1)
            weight_low(3)

            def edge_offsets():
                ve.wait_ge(epre_ready, 1)
                link(V.tensor_copy(e_cnti[:, :], PS[:, 7, 64:64 + NB]))
                link(V.tensor_scalar(e_cnt[:, :], e_cnti[:, :], float(SC - 1), None, ALU.add))
                link(V.tensor_copy(e_cnti[:, :], e_cnt[:, :]))
                link(V.tensor_scalar(e_cnti[:, :], e_cnti[:, :], 9, None, ALU.logical_shift_right))
                link(V.tensor_copy(e_nsc[:, :], e_cnti[:, :]))
                link(V.tensor_tensor_scan(e_end[:, :], ones_c[:, 0:NB], e_nsc[:, :], 0.0, ALU.mult, ALU.add))
                link(V.tensor_tensor(e_base[:, :], e_end[:, :], e_nsc[:, :], ALU.subtract))
                link(V.tensor_scalar(e_base[:, :], e_base[:, :], float(SC), -1.0, ALU.mult, ALU.add))
                link(V.tensor_tensor(e_base[:, :], PS[:, 7, 0:NB], e_base[:, :], ALU.add))
                link(V.memset(e_pos[:, :], 0.0))

            def edge_bucket(b):
                link(V.tensor_scalar(e_mask[:, :], e_bf[:, :], iota_f[0:EP, b:b + 1], None, ALU.is_equal))
                link(V.tensor_tensor_scan(e_cum[:, :], ones_c[0:EP, 0:EC], e_mask[:, :], 0.0, ALU.mult, ALU.add))
                link(V.scalar_tensor_tensor(e_cum[:, :], e_cum[:, :], e_base[0:EP, b:b + 1], e_mask[:, :],
                                            ALU.add, ALU.mult))
                link(V.tensor_tensor(e_pos[:, :], e_pos[:, :], e_cum[:, :], ALU.add))

            def edge_places():
                link(V.tensor_copy(e_tmp[:, :], e_pos[:, :]))
                link(V.tensor_scalar(pos_i[:, :], e_tmp[:, :], 2, P - 1, ALU.logical_shift_right, ALU.bitwise_and))
                link(V.tensor_scalar(pos_i[:, :], pos_i[:, :], float(NCH), None, ALU.mult))
                link(V.tensor_scalar(e_bkt[:, :], e_tmp[:, :], 9, 2, ALU.logical_shift_right, ALU.logical_shift_left))
                link(V.tensor_tensor(pos_i[:, :], pos_i[:, :], e_bkt[:, :], ALU.add))
                link(V.tensor_scalar(e_tmp[:, :], e_tmp[:, :], 3, None, ALU.bitwise_and))
                link(V.tensor_tensor(pos_i[:, :], pos_i[:, :], e_tmp[:, :], ALU.add))
                link(V.tensor_scalar(pairs[:, :, 0], e_dst[:, :], P - 1, None, ALU.bitwise_and))
                V.tensor_copy(pairs[:, :, 1], e_src[:, :]).then_inc(scat_ready, 1)

            def superchunk_offsets():
                link(V.memset(e_acc[:, :], 0.0))
                for b in range(NB):
                    link(V.scalar_tensor_tensor(e_acc[:, :], iota_f[0:1, 0:NSC], e_end[0:1, b:b + 1], e_acc[:, :],
                                                ALU.is_ge, ALU.add))
                link(V.tensor_scalar(e_acc[:, :], e_acc[:, :], float(NB - 1), float(TP), ALU.min, ALU.mult))
                link(V.tensor_copy(bkt_row[:, :], e_acc[:, :]))

            EDGE_J = (NB + 1) // 2
            for j in range(2 * NPAIR):
                f, hi, lo = QF[j % 2], QH[j % 2], QL[j % 2]
                for t, (c0, w) in enumerate(TILES):
                    n, c = NT * j + t, slice(c0, c0 + w)
                    ve.wait_ge(qk_act, n + 1)
                    V.tensor_tensor(lo[:, c], f[:, c], hi[:, c].bitcast(F32), ALU.subtract).then_inc(qk_lo, 1)
                if j == 0:
                    edge_offsets()
                if j < EDGE_J:
                    for b in range(2 * j, min(2 * j + 2, NB)):
                        edge_bucket(b)
                elif j == EDGE_J:
                    edge_places()
                elif j == EDGE_J + 1:
                    superchunk_offsets()

            ve.wait_ge(ks_ps, 1)
            link(V.tensor_scalar(negr[:, :], PS[:, 6, 0:NG], EPS_K, None, ALU.add))
            link(V.reciprocal(negr[:, :], negr[:, :]))
            link(V.tensor_scalar(negr[:, :], negr[:, :], -1.0, None, ALU.mult))

            def first(p):
                return type(p) is int and p == 0

            def neg_step(p, i):
                g = p * (2 * NB) + i
                ve.wait_ge(s_ready, g + 1)
                if not (first(p) and i < 2):
                    ve.wait_ge(p_exp, g - 1)
                V.tensor_scalar(SN[i % 2][:, :], ps_flat[:, 0:T], negr[:, bass.ds(g, 1)], None, ALU.mult, ALU.min,
                                accum_out=negmax[:, i % 2:i % 2 + 1]).then_inc(s_neg, 1)

            def lo_step(p, i):
                g = p * (2 * NB) + i
                q = slice((i % 2) * P, (i % 2 + 1) * P)
                for part, (b0, b1) in enumerate(PARTS):
                    ve.wait_ge(pt_hi, g * 2 + (part + 1))
                    V.tensor_tensor(PT[i // 2 % 2][1][:, b0:b1, q], pt_banks(b0, b1),
                                    PT[i // 2 % 2][0][:, b0:b1, q].bitcast(F32), ALU.subtract).then_inc(pt_lo, 1)

            def att_steps(p):
                for i in range(2 * NB):
                    neg_step(p, i)
                    if i > 0:
                        lo_step(p, i - 1)
                    elif not first(p):
                        lo_step(p - 1, 2 * NB - 1)

            ve.wait_ge(stack_in[0], 80)
            for s in range(2):
                V.memset(PR[s][:, T:TP], 0.0).then_inc(p_pad, 1)
            att_steps(0)
            with ve.Fori(1, NPAIR) as p:
                att_steps(p)
            lo_step(NPAIR - 1, 2 * NB - 1)

            ve.wait_ge(p_exp, NG)
            V.reciprocal(rowsum[:, :], rowsum[:, :]).then_inc(rinv_done, 1)
            ve.wait_ge(wo_hi, 1)
            V.tensor_tensor(WO[1][:, :, :], WO_RAW[:, :, :], WO[0][:, :, :].bitcast(F32), ALU.subtract).then_inc(wo_lo, 1)
            ve.wait_ge(o_out, NG // 2)
            for p in range(NPAIR):
                V.tensor_tensor(OP[:, p, :], OP[:, p, :], OM[:, p, :], ALU.add).then_inc(o_sum, 1)
            for p in range(NPAIR):
                for t, (c0, w) in enumerate(TILES):
                    n, c = NT * p + t, slice(c0, c0 + w)
                    ve.wait_ge(r_ps, n + 1)
                    ve.wait_ge(o_sum, p + 1)
                    V.tensor_tensor(OP[:, p, c], PS[:, n % 4, 0:w], OP[:, p, c], ALU.mult).then_inc(on_f, 1)
                    if n > 0:
                        pp, (cc, ww) = (n - 1) // NT, TILES[(n - 1) % NT]
                        ve.wait_ge(on_hi, n)
                        V.tensor_tensor(ON[1][:, pp, cc:cc + ww], OP[:, pp, cc:cc + ww],
                                        ON[0][:, pp, cc:cc + ww].bitcast(F32), ALU.subtract).then_inc(on_lo, 1)
            cc, ww = TILES[-1]
            ve.wait_ge(on_hi, NPAIR * NT)
            V.tensor_tensor(ON[1][:, NPAIR - 1, cc:cc + ww], OP[:, NPAIR - 1, cc:cc + ww],
                            ON[0][:, NPAIR - 1, cc:cc + ww].bitcast(F32), ALU.subtract).then_inc(on_lo, 1)
            ve.wait_ge(xr_b, 1)
            with ve.Fori(0, NB) as b:
                ve.wait_ge(wo_ps, b + 1)
                V.tensor_tensor(one(ACC[:, bass.ds(b, 1), :]), one(PS[:, bass.ds(b % 4 + 4, 1), :]),
                                one(XR[:, bass.ds(b, 1), :]), ALU.add).then_inc(acc_done, 1)

            ve.wait_ge(on_lo, NPAIR * NT)
            link(V.memset(CT[:, :, :], 0.0))
            for b in range(NB):
                V.tensor_copy(CT[:, b, b * P:(b + 1) * P], ident[:, :]).then_inc(ct_add, 1)
            ve.wait_ge(edges_back, 16)
            V.tensor_copy(e_df[:, :], e_load[:, :, 0])
            link(V.tensor_copy(e_sf[:, :], e_load[:, :, 1]))
            ct_flat = CT[:, :, :].rearrange("p b t -> p (b t)")

            def one_hots(i, par, wait=True):
                if wait:
                    ve.wait_ge(ct_ps, i - 1)
                for j in range(4):
                    col = bass.ds(i * 4 + j, 1)
                    V.tensor_scalar(OHS[4 * par + j][:, :], iota_h[:, :], e_sf[:, col], None, ALU.is_equal)
                    V.tensor_scalar(OHD[4 * par + j][:, :], iota_h[:, 0:P], e_df[:, col], None,
                                    ALU.is_equal).then_inc(oh_ready, 1)

            def add_counts(i, par):
                off = ve.value_load(bkt_row[0:1, bass.ds(i, 1)], min_val=0, max_val=(NB - 1) * TP)
                ve.wait_ge(ct_ps, i + 1)
                ve.wait_ge(ct_add, i + NB)
                V.tensor_tensor(ct_flat[:, bass.ds(off, T)], ps_flat[:, par * 2048:par * 2048 + T],
                                ct_flat[:, bass.ds(off, T)], ALU.add).then_inc(ct_add, 1)

            one_hots(0, 0, wait=False)
            one_hots(1, 1, wait=False)
            add_counts(0, 0)
            one_hots(2, 0)
            add_counts(1, 1)
            with ve.Fori(1, NSC // 2 - 1) as k:
                one_hots(k * 2 + 1, 1)
                add_counts(k * 2, 0)
                one_hots(k * 2 + 2, 0)
                add_counts(k * 2 + 1, 1)
            one_hots(NSC - 1, 1)
            add_counts(NSC - 2, 0)
            add_counts(NSC - 1, 1)
            ve.wait_ge(ct_add, NB + NSC)
            link(V.tensor_reduce(deg[:, :], CT[:, :, :], AX_X, ALU.add))
            rsqrt(dinv[:, :], deg[:, :], NB)
            V.tensor_copy(CTR[:, :, :], CT[:, :, :]).then_inc(ct_ready, 1)
            ve.wait_ge(acc_done, NB)
            V.tensor_copy(deg[:, :], dinv[:, :]).then_inc(dd_ready, 1)

            ve.wait_ge(w2_hi, 1)
            V.tensor_tensor(W2H[1][:, :, :], W2_RAW[:, :, :], W2H[0][:, :, :].bitcast(F32), ALU.subtract).then_inc(w2_lo, 1)
            for b in range(NB):
                V.tensor_scalar(H1[:, b, :], H1[:, b, :], dinv[:, b:b + 1], None, ALU.mult).then_inc(h1_scaled, 1)
            with ve.Fori(0, NB) as b:
                ve.wait_ge(hs_hi, b + 1)
                V.tensor_tensor(HS[1][:, bass.ds(b, 1), :], H1[:, bass.ds(b, 1), :],
                                HS[0][:, bass.ds(b, 1), :].bitcast(F32), ALU.subtract).then_inc(hs_lo, 1)
            ve.wait_ge(dr_done, NT)
            for c in range(KC):
                for t, (c0, w) in enumerate(TILES):
                    n = NT * c + t
                    ve.wait_ge(g_ps, n + 1)
                    V.tensor_tensor(G[:, c, c0:c0 + w], PS[:, n % 4, 0:w], dinv_all[:, c0:c0 + w],
                                    ALU.mult).then_inc(g_done, 1)
                ve.wait_ge(g_done, NT * (c + 1))
                for t, (c0, w) in enumerate(KTILES):
                    last = V.bn_stats(ln_st[:, t, :], G[:, c, c0:c0 + w])
                link(last)
                link(V.bn_aggr(ln_mv[:, c, :], ln_st[:, 0:NT, :].rearrange("p t s -> p (t s)")))
            link(V.tensor_scalar(var_c[:, 0:KC], ln_mv[:, 0:KC, 1], EPS_LN, None, ALU.add))
            rsqrt(rstd[:, 0:KC], var_c[:, 0:KC], KC)
            link(V.tensor_tensor(small[:, 0:KC], gamma_sb[:, :], rstd[:, 0:KC], ALU.mult))
            link(V.tensor_tensor(small[:, KC:2 * KC], ln_mv[:, 0:KC, 0], small[:, 0:KC], ALU.mult))
            V.tensor_tensor(small[:, KC:2 * KC], beta_sb[:, :], small[:, KC:2 * KC], ALU.subtract).then_inc(bn_done, 1)
            for c in range(KC):
                ve.wait_ge(gr_hi, c + 1)
                V.tensor_tensor(GR[1][:, c, :], G[:, c, :], GR[0][:, c, :].bitcast(F32), ALU.subtract).then_inc(gr_lo, 1)

            def h2_bias(b):
                ve.wait_ge(h2_ps, b + 1)
                V.tensor_tensor(one(ht[:, bass.ds(b % 2, 1), :]), one(PS[:, bass.ds(b % 4, 1), :]), b2_all[:, :],
                                ALU.add).then_inc(h2_b, 1)

            def h2_low(b):
                ve.wait_ge(h2_hi, b + 1)
                V.scalar_tensor_tensor(one(H2[1][:, bass.ds(b, 1), :]), one(ht[:, bass.ds(b % 2, 1), :]),
                                       dinv[:, bass.ds(b, 1)], one(H2[0][:, bass.ds(b, 1), :]).bitcast(F32),
                                       ALU.mult, ALU.subtract).then_inc(h2_lo, 1)

            h2_bias(0)
            h2_bias(1)
            h2_low(0)
            with ve.Fori(2, NB) as b:
                ve.wait_ge(h2_lo, b - 1)
                h2_bias(b)
                h2_low(b - 1)
            h2_low(NB - 1)
            with ve.Fori(0, NB) as b:
                ve.wait_ge(a2_ps, b + 1)
                V.scalar_tensor_tensor(one(ACC[:, bass.ds(b, 1), :]), one(PS[:, bass.ds(b % 4 + 4, 1), :]),
                                       dinv[:, bass.ds(b, 1)], one(ACC[:, bass.ds(b, 1), :]),
                                       ALU.mult, ALU.add).then_inc(x2_done, 1)

            ve.wait_ge(x2_done, NB)
            layernorm(ACC, XN, lambda b: None, xn2_ready, [(0, NB)])
            for n, (raw, (hi, lo)) in enumerate(((RW_RAW, RW), (F1_RAW, F1), (F2_RAW, F2))):
                ve.wait_ge(f_hi, n + 1)
                V.tensor_tensor(lo[:, :, :], raw[:, :, :], hi[:, :, :].bitcast(F32), ALU.subtract).then_inc(f_lo, 1)
            with ve.Fori(0, NB) as b:
                ve.wait_ge(x2t_hi, b + 1)
                V.tensor_tensor(X2T[1][:, :, bass.ds(b * P, P)],
                                PS[:, bass.ds(b % 4, 1), :].rearrange("p a (c t) -> p (a c) t", c=KC),
                                X2T[0][:, :, bass.ds(b * P, P)].bitcast(F32), ALU.subtract).then_inc(x2t_lo, 1)
            with ve.Fori(0, NB) as b:
                ve.wait_ge(lg_ps, b + 1)
                V.tensor_copy(one(LG[:, bass.ds(b, 1), :]), PS[:, bass.ds(b % 4 + 4, 1), 0:NE].rearrange("p a e -> p (a e)")
                              ).then_inc(lg_done, 1)
            ve.wait_ge(lg_done, NB)
            for b in range(NB):
                last = V.max(top8[:, b, :], LG[:, b, :])
            link(last)
            for b in range(NB):
                last = V.max_index(idx8[:, b, :], top8[:, b, :], LG[:, b, :])
            link(last)
            V.tensor_scalar(l1neg[:, :], top8[:, :, 0], -1.0, None, ALU.mult).then_inc(top_done, 1)
            link(V.tensor_copy(idxf[:, :, :], idx8[:, :, :]))
            cols = iota_f[:, None, 0:NE].to_broadcast([P, NB, NE])
            V.tensor_tensor(MK[:, :, :], cols, idxf[:, :, 0:1].to_broadcast([P, NB, NE]), ALU.is_equal)
            link(V.tensor_tensor(MR[:, :, :], cols, idxf[:, :, 1:2].to_broadcast([P, NB, NE]), ALU.is_equal))
            link(V.tensor_tensor(MK[:, :, :], MK[:, :, :], MR[:, :, :], ALU.add))
            link(V.memset(MR[:, 0, :], 0.0))
            for b in range(1, NB):
                ins = V.tensor_tensor(MR[:, b, :], MR[:, b - 1, :], MK[:, b - 1, :], ALU.add)
                if b < NB - 1:
                    link(ins)
            ins.then_inc(mk_done, 1)
            ve.wait_ge(ps_pos, 1)
            mk_f, mr_f = (t[:, :, :].rearrange("p b e -> p (b e)") for t in (MK, MR))
            V.scalar_tensor_tensor(mr_f[:, 0:512], PS[:, 4, :], float(CAP), mk_f[:, 0:512], ALU.is_lt, ALU.mult)
            link(V.scalar_tensor_tensor(mr_f[:, 512:NB * NE], PS[:, 5, 0:NB * NE - 512], float(CAP),
                                        mk_f[:, 512:NB * NE], ALU.is_lt, ALU.mult))
            ve.wait_ge(el_done, NB)
            link(V.tensor_tensor(MR[:, :, :], MR[:, :, :], EL[:, :, :], ALU.mult))
            V.reciprocal(zsum[:, :], zsum[:, :])
            link(V.tensor_reduce(gate[:, :], MR[:, :, :], AX_X, ALU.add))
            V.tensor_tensor(gate[:, :], gate[:, :], zsum[:, :], ALU.mult).then_inc(gate_done, 1)
            ve.wait_ge(gate_done, 1)
            for f in range(FC):
                for t, (c0, w) in enumerate(TILES):
                    n = NT * f + t
                    ve.wait_ge(u_hi, n + 1)
                    V.tensor_tensor(HFH[1][:, f, c0:c0 + w], HF[:, f, c0:c0 + w], HFH[0][:, f, c0:c0 + w].bitcast(F32),
                                    ALU.subtract).then_inc(u_lo, 1)
            ve.wait_ge(f_in, 64)
            for b in range(NB):
                ve.wait_ge(y_ps, b + 1)
                V.tensor_tensor(yt[:, :], PS[:, 4 + b % 4, :], fb2_all[:, :], ALU.add).then_inc(y_b, 1)
                ve.wait_ge(y_b, b + 1)
                V.scalar_tensor_tensor(ACC[:, b, :], yt[:, :], gate[:, b:b + 1], ACC[:, b, :],
                                       ALU.mult, ALU.add).then_inc(y_done, 1)
                ve.wait_ge(y_done, b + 1)

        @block.tensor
        def _(pe):
            MM = nc.tensor.matmul

            def product(out_t, pairs_t):
                steps = [(a[i], b[j]) for a, b in pairs_t for i, j in ((0, 0), (0, 1), (1, 0))]
                for s, (l, r) in enumerate(steps):
                    last = MM(out_t, l, r, start=s == 0, stop=s == len(steps) - 1)
                return last

            pe.wait_ge(const_done, 1)
            pe.wait_ge(etot_ready, NB)
            MM(PS[:, 7, 0:NB], before[0:EP, :], e_tot[0:EP, :], start=True, stop=True)
            MM(PS[:, 7, 64:64 + NB], mask_a[0:EP, :], e_tot[0:EP, :], start=True, stop=False)
            MM(PS[:, 7, 64:64 + NB], mask_b[0:EP, :], e_tot[0:EP, :], start=False, stop=True).then_inc(epre_ready, 1)
            def transpose_x(b):
                pe.wait_ge(xn_ready, b + 1)
                if b >= 2:
                    pe.wait_ge(xt_lo, b - 1)
                for c in range(KC):
                    last = nc.tensor.transpose(PS[:, b % 2, c * P:(c + 1) * P], X[:, b, c * P:(c + 1) * P], ident[:, :])
                last.then_inc(xt_ps, 1)

            transpose_x(0)
            transpose_x(1)
            for b in range(NB):
                pe.wait_ge(xt_lo, b + 1)
                for n, (ready, used) in enumerate(((v_ps, v_biased), (h1_ps, h1_done))):
                    if b == 0:
                        pe.wait_ge(w_lo, n + 1)
                    if b >= 2:
                        pe.wait_ge(used, b - 1)
                    product(PS[:, 2 + 2 * n + b % 2, :], [([XT[l][:, c, blk(b)] for l in range(2)],
                                                           [WH[n][l][:, c, :] for l in range(2)])
                                                          for c in range(KC)]).then_inc(ready, 1)
                if b + 2 < NB:
                    transpose_x(b + 2)
            pe.wait_ge(v_biased, NB)

            def key_sums(j):
                pe.wait_ge(qk_act, NT * (j + 1))
                for b in range(NB):
                    g = 2 * NB * (j - NPAIR) + b
                    last = MM(PS[:, 6, g:g + NB + 1:NB], QF[j % 2][:, blk(b)], head_ones[:, DH - 1:DH + 1],
                              start=True, stop=True)
                if j == 2 * NPAIR - 1:
                    last.then_inc(ks_ps, 1)
                else:
                    last.then_inc(ks_read, 1)

            for j in range(2 * NPAIR):
                if j % NPAIR == 0:
                    pe.wait_ge(w_lo, 3 + j // NPAIR)
                wh = WH[j // NPAIR]
                for t, (c0, w) in enumerate(TILES):
                    n = NT * j + t
                    if n >= 4:
                        pe.wait_ge(qk_act, n - 3)
                    product(PS[:, n % 4, 0:w], [([wh[l][:, c, blk(j % NPAIR)] for l in range(2)],
                                                     [XT[l][:, c, c0:c0 + w] for l in range(2)])
                                                    for c in range(KC)]).then_inc(qk_ps, 1)
                if j > NPAIR:
                    key_sums(j - 1)
            key_sums(2 * NPAIR - 1)

            def first(p):
                return type(p) is int and p == 0

            def scores(p, i):
                s = i // NB
                if i % NB == 0:
                    pe.wait_ge(stack_in[s], (p + 1) * 80)
                if not (first(p) and i == 0):
                    pe.wait_ge(s_neg, p * (2 * NB) + i)
                for part in range(2):
                    for t, (c0, w) in enumerate(KTILES):
                        last = MM(PS[:, t, 0:w], QS[s][:, part, blk(i % NB)], KS[s][:, c0:c0 + w],
                                  start=part == 0, stop=part == 1)
                last.then_inc(s_ready, 1)

            def transposes(p, i):
                g = p * (2 * NB) + i
                pe.wait_ge(p_exp, g + 1)
                for part, (b0, b1) in enumerate(PARTS):
                    if not (first(p) and i == 0):
                        pe.wait_ge(pt_lo, g * 2 - (1 - part))
                    for b in range(b0, b1):
                        last = nc.tensor.transpose(PS[:, 3 + b // 4, b % 4 * P:(b % 4 + 1) * P], PR[i % 2][:, blk(b)],
                                                   ident[:, :])
                    last.then_inc(pt_ps, 1)

            def values(p, k, half):
                if half == 0:
                    pe.wait_ge(pt_lo, p * (4 * NB) + 4 * (k + 1))
                    if not (first(p) and k < 2):
                        pe.wait_ge(o_out, p * NB + k - 1)
                for b in range(half * NB // 2, (half + 1) * NB // 2):
                    for part in range(2):
                        last = MM(PS[:, 6 + k % 2, 0:2 * P], VS[k // (NB // 2)][:, b, :], PT[k % 2][part][:, b, :],
                                  start=b == 0 and part == 0, stop=b == NB - 1 and part == 1)
                if half == 1:
                    last.then_inc(av_done, 1)

            def att_steps(p):
                for i in range(2 * NB):
                    scores(p, i)
                    if i > 0:
                        transposes(p, i - 1)
                    elif not first(p):
                        transposes(p - 1, 2 * NB - 1)
                    k, half = ((i - 3) // 2, 0) if i % 2 else ((i - 4) // 2, 1)
                    if k >= 0:
                        values(p, k, half)
                    elif not first(p):
                        values(p - 1, k + NB, half)

            pe.wait_ge(p_pad, 2)
            att_steps(0)
            with pe.Fori(1, NPAIR) as p:
                att_steps(p)
            transposes(NPAIR - 1, 2 * NB - 1)
            values(NPAIR - 1, NB - 2, 1)
            values(NPAIR - 1, NB - 1, 0)
            values(NPAIR - 1, NB - 1, 1)

            for p in range(NPAIR):
                pe.wait_ge(diag_done, 2 * (p + 1))
                for t, (c0, w) in enumerate(TILES):
                    n, tb = NT * p + t, slice(c0 // P, (c0 + w) // P)
                    if n >= 4:
                        pe.wait_ge(on_f, n - 3)
                    else:
                        pe.wait_ge(pt_lo, 2 * NG)
                    for s, mask in enumerate((mask_a, mask_b)):
                        last = MM(PS[:, n % 4, 0:w], mask[:, :], DG[s][:, tb, :].rearrange("p b t -> p (b t)"),
                                  start=s == 0, stop=s == 1)
                    last.then_inc(r_ps, 1)
            pe.wait_ge(wo_lo, 1)
            pe.wait_ge(on_lo, NPAIR * NT)
            pe.wait_ge(o_out, NG // 2)
            for b in range(NB):
                if b >= 4:
                    pe.wait_ge(acc_done, b - 3)
                product(PS[:, 4 + b % 4, :], [([ON[l][:, c, blk(b)] for l in range(2)], [WO[l][:, c, :] for l in range(2)])
                                              for c in range(KC)]).then_inc(wo_ps, 1)

            def counts(i, par, wait=True):
                if wait:
                    pe.wait_ge(ct_add, i + NB - 1)
                for j in range(4):
                    pe.wait_ge(oh_ready, i * 4 + (j + 1))
                    for t, (c0, w) in enumerate(KTILES):
                        last = MM(PS[:, 4 * par + t, 0:w], OHD[4 * par + j][:, :], OHS[4 * par + j][:, c0:c0 + w],
                                  start=j == 0, stop=j == 3)
                last.then_inc(ct_ps, 1)

            pe.wait_ge(acc_done, NB)
            with pe.Fori(0, NSC // 2) as k:
                counts(k * 2, 0)
                counts(k * 2 + 1, 1)

            pe.wait_ge(diag_done, 2 * NPAIR + 1)
            for t, (c0, w) in enumerate(TILES):
                tb = slice(c0 // P, (c0 + w) // P)
                for s, mask in enumerate((mask_a, mask_b)):
                    last = MM(PS[:, t, 0:w], mask[:, :], DGD[:, tb, :].rearrange("p b t -> p (b t)"),
                              start=s == 0, stop=s == 1)
                last.then_inc(dr_ps, 1)
            pe.wait_ge(ct_ready, 1)
            pe.wait_ge(hs_lo, NB)
            pe.wait_ge(dr_done, NT)
            for c in range(KC):
                for t, (c0, w) in enumerate(TILES):
                    n = NT * c + t
                    if n >= 4:
                        pe.wait_ge(g_done, n - 3)
                    for b in range(NB):
                        for l in range(2):
                            last = MM(PS[:, n % 4, 0:w], HS[l][:, b, c * P:(c + 1) * P], CTR[:, b, c0:c0 + w],
                                      start=b == 0 and l == 0, stop=b == NB - 1 and l == 1)
                    last.then_inc(g_ps, 1)
            pe.wait_ge(w2_lo, 1)
            pe.wait_ge(gr_lo, KC)
            for b in range(NB):
                if b >= 4:
                    pe.wait_ge(h2_b, b - 3)
                product(PS[:, b % 4, :], [([GR[l][:, c, blk(b)] for l in range(2)], [W2H[l][:, c, :] for l in range(2)])
                                          for c in range(KC)]).then_inc(h2_ps, 1)
            pe.wait_ge(h2_lo, NB)
            for b in range(NB):
                if b >= 4:
                    pe.wait_ge(x2_done, b - 3)
                for d in range(NB):
                    for l in range(2):
                        last = MM(PS[:, 4 + b % 4, :], CTR[:, d, blk(b)], H2[l][:, d, :],
                                  start=d == 0 and l == 0, stop=d == NB - 1 and l == 1)
                last.then_inc(a2_ps, 1)

            for b in range(NB):
                pe.wait_ge(xn2_ready, b + 1)
                if b >= 4:
                    pe.wait_ge(x2t_lo, b - 3)
                for c in range(KC):
                    last = nc.tensor.transpose(PS[:, b % 4, c * P:(c + 1) * P], XN[:, b, c * P:(c + 1) * P], ident[:, :])
                last.then_inc(x2t_ps, 1)
            pe.wait_ge(x2t_lo, NB)
            pe.wait_ge(f_lo, 3)
            for b in range(NB):
                if b >= 4:
                    pe.wait_ge(lg_done, b - 3)
                product(PS[:, 4 + b % 4, 0:NE], [([X2T[l][:, c, blk(b)] for l in range(2)],
                                                  [RW[l][:, c, :] for l in range(2)]) for c in range(KC)]).then_inc(lg_ps, 1)
            for f in range(FC):
                for t, (c0, w) in enumerate(TILES):
                    n = NT * f + t
                    if n >= 4:
                        pe.wait_ge(u_gelu, n - 3)
                    product(PS[:, n % 4, 0:w], [([F1[l][:, c, blk(f)] for l in range(2)],
                                                 [X2T[l][:, c, c0:c0 + w] for l in range(2)])
                                                for c in range(KC)]).then_inc(u_ps, 1)
            pe.wait_ge(mk_done, 1)
            mk_f, mr_f = (t[:, :, :].rearrange("p b e -> p (b e)") for t in (MK, MR))
            for bank, c in ((4, slice(0, 512)), (5, slice(512, NB * NE))):
                w = c.stop - c.start
                MM(PS[:, bank, 0:w], before[:, :], mk_f[:, c], start=True, stop=False)
                MM(PS[:, bank, 0:w], mask_a[:, :], mr_f[:, c], start=False, stop=False)
                last = MM(PS[:, bank, 0:w], mask_b[:, :], mr_f[:, c], start=False, stop=True)
            last.then_inc(ps_pos, 1)
            pe.wait_ge(u_lo, FC * NT)
            pe.wait_ge(gate_done, 1)
            for b in range(NB):
                if b >= 4:
                    pe.wait_ge(y_b, b - 3)
                product(PS[:, 4 + b % 4, :], [([HFH[l][:, f, blk(b)] for l in range(2)], [F2[l][:, f, :] for l in range(2)])
                                              for f in range(FC)]).then_inc(y_ps, 1)


_TRANSPOSED = {'L0_mix_Wq', 'L0_mix_Wk', 'L0_mix_Wv', 'L0_mix_Wo', 'L0_ffn_router_w', 'L0_ffn_w1', 'L0_ffn_w2'}
_INS = ['x', 'src', 'dst', 'L0_gnn_W1', 'L0_gnn_b1', 'L0_gnn_gamma', 'L0_gnn_beta', 'L0_gnn_W2', 'L0_gnn_b2',
        'L0_mix_Wq', 'L0_mix_bq', 'L0_mix_Wk', 'L0_mix_bk', 'L0_mix_Wv', 'L0_mix_bv', 'L0_mix_Wo', 'L0_mix_bo',
        'L0_ffn_router_w', 'L0_ffn_w1', 'L0_ffn_b1', 'L0_ffn_w2', 'L0_ffn_b2']


def kernel(**inputs):
    import numpy as _np
    import concourse.bacc as _bacc
    from concourse import mybir as _mybir
    from concourse.bass_utils import run_bass_kernel_spmd as _run

    nc = _bacc.Bacc("TRN2", target_bir_lowering=False, num_devices=1)
    arrays, args = {}, []
    for name in _INS:
        a = _np.asarray(inputs[name])
        a = _np.ascontiguousarray(a.T if name in _TRANSPOSED else a)
        arrays[f"in_{name}_dram"] = a
        args.append(nc.dram_tensor(f"in_{name}_dram", a.shape, _mybir.dt.from_np(a.dtype), kind="ExternalInput").ap())
    x = inputs['x']
    out = nc.dram_tensor("out_0_dram", x.shape, _mybir.dt.float32, kind="ExternalOutput").ap()
    gps_layer(nc, *args, out)
    r = _run(nc, [arrays], core_ids=[0])
    return r.results[0]["out_0_dram"]
```

```python
from contextlib import ExitStack

import concourse.bass as bass
from concourse import mybir

F32 = mybir.dt.float32
F32R = mybir.dt.float32r
BF16 = mybir.dt.bfloat16
FP16 = mybir.dt.float16
I32 = mybir.dt.int32
U32 = mybir.dt.uint32
ALU = mybir.AluOpType
ACT = mybir.ActivationFunctionType
AX_X = mybir.AxisListType.X

P = 128
KIB = 1024


class Chain:

    def __init__(self, eng, sem):
        self.eng, self.sem, self.n = eng, sem, 0

    def __call__(self, ins):
        self.n = self.n + 1
        ins.then_inc(self.sem, 1)
        self.eng.wait_ge(self.sem, self.n)


def gps_layer(nc, x, src, dst, W1, b1, gamma, beta, W2, b2, WqT, bq, WkT, bk, WvT, bv, WoT, bo,
              rwT, w1T, fb1, w2T, fb2, out):
    T, D = x.shape
    NB = -(-T // P)
    TP = NB * P
    LAST = T - (NB - 1) * P
    KC = D // P
    H = 8
    DH = D // H
    NPAIR = H // 2
    TILES = [(c, min(512, TP - c)) for c in range(0, TP, 512)]
    KTILES = [(c, min(512, T - c)) for c in range(0, T, 512)]
    CW = T + 1
    CTILES = [(c, min(512, CW - c)) for c in range(0, CW, 512)]
    NT = len(TILES)
    E = src.shape[0]
    EP = max(p for p in range(1, P + 1) if E % p == 0)
    EC = E // EP
    SC = 4 * P
    NSC = -(-E // SC) + NB
    NSC += NSC % 2
    NCH = 4 * NSC
    NE = rwT.shape[1]
    F = w1T.shape[1]
    FC = F // P
    CAP = 512
    NG = H * NB
    EPS_K, EPS_LN = 1e-6, 1e-5

    q_dram = nc.dram_tensor("q_scratch", [2, D, TP], F32, kind="Internal").ap()
    k_dram = nc.dram_tensor("k_scratch", [2, D, TP], F32, kind="Internal").ap()
    v_dram = nc.dram_tensor("v_scratch", [P, H, NB * P], F32, kind="Internal").ap()
    e_dram = nc.dram_tensor("edge_scratch", [P * NCH, 2], I32, kind="Internal").ap()

    with ExitStack() as ctx:
        def sb(name, shape, dt):
            return ctx.enter_context(nc.sbuf_tensor(name, shape, dt))

        def sem(name):
            return ctx.enter_context(nc.semaphore(name))

        ident = sb("ident", [P, P], F32)
        ones_m = sb("ones_m", [P, P], F32)
        mask_a = sb("mask_a", [P, P], F32)
        mask_b = sb("mask_b", [P, P], F32)
        head_ones = sb("head_ones", [P, P], F32)
        before = sb("before", [P, P], F32)
        iota_f = sb("iota_f", [P, P], F32)
        iota_d = sb("iota_d", [P, P], FP16)
        iota_s = sb("iota_s", [P, TP], FP16)
        ln_mv = sb("ln_mv", [P, NB, 2], F32)
        ln_st = sb("ln_st", [P, NB, 6], F32)
        rstd = sb("rstd", [P, NB], F32)
        nt_a = sb("nt_a", [P, NB], F32)
        nt_i = sb("nt_i", [P, NB], I32)
        rowsum = sb("rowsum", [P, NG], F32)
        negr = sb("negr", [P, NG], F32)
        negmax = sb("negmax", [P, 2], F32)
        dinv = sb("dinv", [P, NB], F32)
        deg = sb("deg", [P, NB], F32)
        dinv_half = sb("dinv_half", [P, NB], F32)
        var_c = sb("var_c", [P, NB], F32)
        bq_sb = sb("bq_sb", [P, KC], F32)
        bk_sb = sb("bk_sb", [P, KC], F32)
        gamma_sb = sb("gamma_sb", [P, KC], F32)
        beta_sb = sb("beta_sb", [P, KC], F32)
        fb1_sb = sb("fb1_sb", [P, FC], F32)
        pos_i = sb("pos_i", [EP, EC], I32)
        pairs = sb("pairs", [EP, EC, 2], I32)
        bkt_row = sb("bkt_row", [1, NSC], I32)
        small = sb("small", [P, 2 * KC], F32)
        top8 = sb("top8", [P, NB, 8], F32)
        idx8 = sb("idx8", [P, NB, 8], U32)

        arena_base = -(-nc.sbuf_base // 64) * 64

        def at(name, kib, shape, dt):
            return nc.alloc_sbuf_tensor_at(name, shape, dt, offset=arena_base + int(kib * KIB))

        H1 = at("H1", 177, [P, NB, D], F32)
        VV = at("VV", 0, [P, H, NB, P], F32R)
        XT = [at("xt_hi", 40, [P, KC, TP], F32R), at("xt_lo", 60, [P, KC, TP], F32R)]
        WH = [[at(f"w{r}_{'hl'[k]}", 80 + 16 * r + 8 * k, [P, KC, D], F32R) for k in range(2)] for r in range(2)]
        WRAW = [at(f"wraw{r}", 112 + 8 * r, [P, KC, D], F32) for r in range(2)]
        X = at("X", 128, [P, NB, D], F32)
        QF = [at(f"qf{r}", 128 + 15 * r, [P, TP], F32) for r in range(2)]
        QH = [at(f"qh{r}", 133 + 15 * r, [P, TP], F32R) for r in range(2)]
        QL = [at(f"ql{r}", 138 + 15 * r, [P, TP], F32R) for r in range(2)]
        bv_all = at("bv_all", 158, [P, D], F32)
        b1_all = at("b1_all", 160, [P, D], F32)
        vt = at("vt", 162, [P, 2, D], F32)
        ones_c = at("ones_c", 166, [P, 512], F32)
        e_src = at("e_src", 168, [EP, EC], I32)
        e_dst = at("e_dst", 168.75, [EP, EC], I32)
        e_bkt = at("e_bkt", 169.5, [EP, EC], I32)
        e_bf = at("e_bf", 170.25, [EP, EC], F32)
        e_mask = at("e_mask", 171, [EP, EC], F32)
        e_cum = at("e_cum", 171.75, [EP, EC], F32)
        e_pos = at("e_pos", 172.5, [EP, EC], F32)
        e_tmp = at("e_tmp", 173.25, [EP, EC], I32)
        e_tot = at("e_tot", 174, [P, NB], F32)
        e_base = at("e_base", 174.125, [P, NB], F32)
        e_cnt = at("e_cnt", 174.25, [P, NB], F32)
        e_cnti = at("e_cnti", 174.375, [P, NB], I32)
        e_end = at("e_end", 174.5, [P, NB], F32)
        e_nsc = at("e_nsc", 174.625, [P, NB], F32)
        e_acc = at("e_acc", 174.75, [1, NSC], F32)
        e_fill = at("e_fill", 175, [P, NCH * 2 // 4], I32)
        QS = [at(f"qs{r}", 0 + 20 * r, [P, 2, TP], F32R) for r in range(2)]
        KS = [at(f"ks{r}", 10 + 20 * r, [P, TP], F32R) for r in range(2)]
        VS = [at(f"vs{r}", 15 + 20 * r, [P, NB, P], F32R) for r in range(2)]
        PT = [[at(f"pt{r}{'hl'[k]}", 40 + 20 * r + 10 * k, [P, NB, 2 * P], F32R) for k in range(2)] for r in range(2)]
        SN = [at(f"sn{r}", 80 + 5 * r, [P, T], F32) for r in range(2)]
        PR = [at(f"pr{r}", 90 + 5 * r, [P, TP], F32) for r in range(2)]
        OP = at("OP", 100, [P, NPAIR, TP], F32)
        OM = at("OM", 120, [P, NPAIR, TP], F32)
        ON = [at("on_hi", 40, [P, NPAIR, TP], F32R), at("on_lo", 60, [P, NPAIR, TP], F32R)]
        WO = [at("wo_hi", 0, [P, KC, D], F32R), at("wo_lo", 8, [P, KC, D], F32R)]
        WO_RAW = at("wo_raw", 140, [P, KC, D], F32)
        bo_all = at("bo_all", 148, [P, D], F32)
        head_rows = at("head_rows", 155, [P, D], F32)
        sums_t = at("sums_t", 80, [H, TP], F32)
        ACC = at("ACC", 157, [P, NB, D], F32)
        CT = at("CT", 105, [P, NB, TP], F32)
        CTR = at("CTR", 105, [P, NB, TP], F32R)
        OHS = [at(f"ohs{r}", 80 + 2.5 * r, [P, TP], BF16) for r in range(8)]
        OHD = [at(f"ohd{r}", 28 + r, [P, 4, P], BF16) for r in range(2)]
        e_load = at("e_load", 24, [P, NCH, 2], I32)
        e_df = at("e_df", 26, [P, NCH], F32)
        e_half = at("e_half", 16, [P, NCH], F32)
        e_sf = at("e_sf", 27, [P, NCH], F32)
        HS = [at("hs_hi", 60, [P, NB, D], F32R), at("hs_lo", 80, [P, NB, D], F32R)]
        G = at("G", 16, [P, KC, TP], F32)
        roots_t = at("roots_t", 100, [1, TP], F32)
        dinv_all = at("dinv_all", 36, [P, TP], F32)
        GR = [at("gr_hi", 177, [P, KC, TP], F32R), at("gr_lo", 16, [P, KC, TP], F32R)]
        W2H = [at("w2_hi", 0, [P, KC, D], F32R), at("w2_lo", 8, [P, KC, D], F32R)]
        W2_RAW = at("w2_raw", 42, [P, KC, D], F32)
        b2_all = at("b2_all", 50, [P, D], F32)
        ht = at("ht", 52, [P, 2, D], F32)
        H2 = [at("h2_hi", 60, [P, NB, D], F32R), at("h2_lo", 80, [P, NB, D], F32R)]
        XN = [at(f"xn{r}", kib, [P, D], F32) for r, kib in enumerate((36, 38, 3, 5))]
        X2T = [at("x2t_hi", 177, [P, KC, TP], F32R), at("x2t_lo", 40, [P, KC, TP], F32R)]
        RW_RAW = at("rw_raw", 0, [P, KC, NE], F32)
        RW = [at("rw_hi", 1, [P, KC, NE], F32R), at("rw_lo", 2, [P, KC, NE], F32R)]
        F1_RAW = at("f1_raw", 3, [P, KC, F], F32)
        F1 = [at("f1_hi", 7, [P, KC, F], F32R), at("f1_lo", 11, [P, KC, F], F32R)]
        F2_RAW = at("f2_raw", 15, [P, FC, D], F32)
        F2 = [at("f2_hi", 19, [P, FC, D], F32R), at("f2_lo", 23, [P, FC, D], F32R)]
        fb2_row = at("fb2_row", 27, [1, D], F32)
        FB2 = [at("fb2_hi", 15, [1, D], F32R), at("fb2_lo", 17, [1, D], F32R)]
        LG = at("LG", 100, [P, NB, NE], F32)
        EL = at("EL", 102.5, [P, NB, NE], F32)
        MK = at("MK", 29, [P, NB, NE], F32)
        MR = at("MR", 31.5, [P, NB, NE], F32)
        ones_r = at("ones_r", 35, [1, P], F32R)
        gate = at("gate", 34, [P, NB], F32)
        zsum = at("zsum", 34.125, [P, NB], F32)
        l1neg = at("l1neg", 34.25, [P, NB], F32)
        idxf = at("idxf", 34.5, [P, NB, 8], F32)
        HF = at("HF", 105, [P, FC, TP], F32)
        HFH = [at("hf_hi", 115, [P, FC, TP], F32R), at("hf_lo", 125, [P, FC, TP], F32R)]

        PS = ctx.enter_context(nc.psum_tensor("PS", [P, 8, 512], F32))
        ps_flat = PS[:, :, :].rearrange("p a b -> p (a b)")

        const_done = sem("const_done")
        x_pad = sem("x_pad")
        x_in = [sem(f"x_in{b}") for b in range(NB)]
        bias_in = sem("bias_in")
        edge_in = sem("edge_in")
        w_in = [sem(f"w_in{n}") for n in range(4)]
        w_hi = sem("w_hi")
        w_lo = sem("w_lo")
        dve = sem("dve_step")
        pool = sem("pool_step")
        fill_set = sem("fill_set")
        fill_out = sem("fill_out")
        etot_ready = sem("etot_ready")
        epre_ready = sem("epre_ready")
        scat_ready = sem("scat_ready")
        scat_done = sem("scat_done")
        edges_back = sem("edges_back")
        xn_ready = sem("xn_ready")
        xt_ps = sem("xt_ps")
        xt_hi = sem("xt_hi")
        xt_lo = sem("xt_lo")
        v_ps = sem("v_ps")
        v_biased = sem("v_biased")
        v_hi = sem("v_hi")
        v_lo = sem("v_lo")
        v_out = sem("v_out")
        h1_ps = sem("h1_ps")
        h1_done = sem("h1_done")
        qk_ps = sem("qk_ps")
        qk_act = sem("qk_act")
        qk_lo = sem("qk_lo")
        ks_ps = sem("ks_ps")
        ks_read = sem("ks_read")
        qk_out = [sem("qk_out0"), sem("qk_out1")]
        stack_in = [sem("stack_in0"), sem("stack_in1")]
        s_ready = sem("s_ready")
        s_neg = sem("s_neg")
        p_exp = sem("p_exp")
        p_pad = sem("p_pad")
        pt_ps = sem("pt_ps")
        pt_hi = sem("pt_hi")
        pt_lo = sem("pt_lo")
        av_done = sem("av_done")
        o_out = sem("o_out")
        rinv_done = sem("rinv_done")
        edges_placed = sem("edges_placed")
        rt_ps = sem("rt_ps")
        head_rows_done = sem("head_rows_done")
        rt_done = sem("rt_done")
        o_sum = sem("o_sum")
        r_ps = sem("r_ps")
        on_f = sem("on_f")
        on_hi = sem("on_hi")
        on_lo = sem("on_lo")
        wo_in = sem("wo_in")
        wo_hi = sem("wo_hi")
        wo_lo = sem("wo_lo")
        xr_in = sem("xr_in")
        xr_b = sem("xr_b")
        wo_ps = sem("wo_ps")
        acc_done = sem("acc_done")
        e_ready = sem("e_ready")
        oh_dve = sem("oh_dve")
        oh_pool = sem("oh_pool")
        oh_act = sem("oh_act")
        ct_ps = sem("ct_ps")
        ct_add = sem("ct_add")
        ct_ready = sem("ct_ready")
        deg_done = sem("deg_done")
        dd_ready = sem("dd_ready")
        dr_ps = sem("dr_ps")
        dr_done = sem("dr_done")
        hs_hi = sem("hs_hi")
        hs_lo = sem("hs_lo")
        g_ps = sem("g_ps")
        g_done = sem("g_done")
        bn_done = sem("bn_done")
        gr_relu = sem("gr_relu")
        gr_lo = sem("gr_lo")
        w2_in = sem("w2_in")
        w2_hi = sem("w2_hi")
        w2_lo = sem("w2_lo")
        h2_ps = sem("h2_ps")
        h2_b = sem("h2_b")
        h2_hi = sem("h2_hi")
        h2_lo = sem("h2_lo")
        a2_ps = sem("a2_ps")
        x2_done = sem("x2_done")
        xn2_ready = sem("xn2_ready")
        x2t_ps = sem("x2t_ps")
        x2t_hi = sem("x2t_hi")
        x2t_lo = sem("x2t_lo")
        f_in = sem("f_in")
        f_hi = sem("f_hi")
        f_lo = sem("f_lo")
        lg_ps = sem("lg_ps")
        el_done = sem("el_done")
        mk_done = sem("mk_done")
        ps_pos = sem("ps_pos")
        u_ps = sem("u_ps")
        u_gelu = sem("u_gelu")
        u_hi = sem("u_hi")
        u_lo = sem("u_lo")
        y_ps = sem("y_ps")
        y_done = sem("y_done")
        out_done = sem("out_done")

        block = ctx.enter_context(nc.Block())

        def blk(b):
            return slice(b * P, (b + 1) * P)

        PARTS = [(0, 4), (4, NB)]

        def pt_banks(b0, b1):
            return ps_flat[:, 3 * 512 + b0 * P:3 * 512 + b1 * P].rearrange("p (b t) -> p b t", b=b1 - b0)

        def row_bcast(v):
            return v.rearrange("(a n) -> a n", a=1).to_broadcast([P, v.shape[0]])

        def w_view(w):
            return w.rearrange("(c p) n -> p c n", p=P)

        @block.sync
        def _(sp):
            sp.dma_start(e_dst[:, :], dst.rearrange("(p c) -> p c", p=EP)).then_inc(edge_in, 16)
            sp.dma_start(e_src[:, :], src.rearrange("(p c) -> p c", p=EP)).then_inc(edge_in, 16)
            for b in range(NB - 1):
                sp.dma_start(X[:, b, :], x[blk(b), :]).then_inc(x_in[b], 16)
            sp.wait_ge(x_pad, 1)
            sp.dma_start(X[0:LAST, NB - 1, :], x[(NB - 1) * P:T, :]).then_inc(x_in[NB - 1], 16)
            sp.dma_start(WRAW[0][:, :, :], w_view(WvT)).then_inc(w_in[0], 16)
            sp.dma_start(WRAW[1][:, :, :], w_view(W1)).then_inc(w_in[1], 16)
            sp.dma_start(bv_all[:, :], row_bcast(bv)).then_inc(bias_in, 16)
            sp.dma_start(b1_all[:, :], row_bcast(b1)).then_inc(bias_in, 16)
            with nc.allow_non_contiguous_dma(reason="biases, one element per partition"):
                for tile, vec in ((bq_sb, bq), (bk_sb, bk), (gamma_sb, gamma), (beta_sb, beta), (fb1_sb, fb1)):
                    sp.dma_start(tile[:, :], vec.rearrange("(c p) -> p c", p=P)).then_inc(bias_in, 16)
            sp.wait_ge(fill_set, 1)
            for r in range(4):
                sp.dma_start(e_dram.rearrange("(p c) t -> p (c t)", p=P)[:, r * (NCH // 2):(r + 1) * (NCH // 2)],
                             e_fill[:, :]).then_inc(fill_out, 16)
            for r, w in enumerate((WqT, WkT)):
                sp.wait_ge(w_lo, r + 1)
                sp.dma_start(WRAW[r][:, :, :], w_view(w)).then_inc(w_in[2 + r], 16)
            def load_head(h, slot):
                rows = bass.ds(h * DH, DH)
                for half in range(2):
                    part = slice(half * DH, (half + 1) * DH)
                    sp.dma_start(QS[slot][part, :, :].bitcast(F32),
                                 q_dram[:, rows, :].rearrange("l d t -> d l t")).then_inc(stack_in[slot], 16)
                    sp.dma_start(KS[slot][part, :].bitcast(F32), k_dram[half, rows, :]).then_inc(stack_in[slot], 16)
                sp.dma_start(VS[slot][:, :, :].bitcast(F32).rearrange("p b d -> p (b d)"),
                             v_dram[:, bass.ds(h, 1), :].rearrange("p a n -> p (a n)")).then_inc(stack_in[slot], 16)

            sp.wait_ge(v_lo, NB)
            sp.dma_start(v_dram, VV[:, :, :, :].bitcast(F32).rearrange("p h b d -> p h (b d)")).then_inc(v_out, 16)
            for j in range(2 * NPAIR):
                sp.wait_ge(qk_lo, NT * (j + 1))
                pr, d = j % NPAIR, (q_dram if j < NPAIR else k_dram)
                sp.dma_start(d[0, blk(pr), :], QH[j % 2][:, :].bitcast(F32)).then_inc(qk_out[j % 2], 16)
                sp.dma_start(d[1, blk(pr), :], QL[j % 2][:, :].bitcast(F32)).then_inc(qk_out[j % 2], 16)
                if j == NPAIR + 1:
                    sp.wait_ge(v_out, 16)
                    sp.wait_ge(qk_out[0], 32 * (NPAIR // 2 + 1))
                    load_head(0, 0)
                    load_head(1, 1)
            sp.wait_ge(qk_out[0], 32 * NPAIR)
            sp.wait_ge(qk_out[1], 32 * NPAIR)
            with sp.Fori(1, NPAIR) as p:
                for s in range(2):
                    sp.wait_ge(av_done, (p - 1) * NB + (s + 1) * (NB // 2))
                    load_head(p * 2 + s, s)
            sp.wait_ge(av_done, NG // 2)
            sp.wait_ge(scat_done, 16 * EC)
            sp.dma_start(e_load[:, :, :].rearrange("p c t -> p (c t)"),
                         e_dram.rearrange("(p c) t -> p (c t)", p=P)).then_inc(edges_back, 16)
            sp.wait_ge(acc_done, NB)
            sp.dma_start(W2_RAW[:, :, :], w_view(W2)).then_inc(w2_in, 16)
            sp.dma_start(b2_all[:, :], row_bcast(b2)).then_inc(w2_in, 16)
            sp.wait_ge(h2_ps, NB)
            sp.dma_start(RW_RAW[:, :, :], w_view(rwT)).then_inc(f_in, 16)
            sp.dma_start(F1_RAW[:, :, :], w_view(w1T)).then_inc(f_in, 16)
            sp.dma_start(F2_RAW[:, :, :], w_view(w2T)).then_inc(f_in, 16)
            sp.dma_start(fb2_row[:, :], fb2.rearrange("(a n) -> a n", a=1)).then_inc(f_in, 16)
            for b in range(NB):
                n = P if b < NB - 1 else LAST
                sp.wait_ge(y_done, b + 1)
                sp.dma_start(out[b * P:b * P + n, :], ACC[0:n, b, :]).then_inc(out_done, 16)
            sp.wait_ge(out_done, 16 * NB)

        @block.gpsimd
        def _(gp):
            link = Chain(gp, pool)
            nc.gpsimd.memset(X[:, NB - 1, :], 0.0).then_inc(x_pad, 1)
            nc.gpsimd.memset(e_fill[:, :], -1).then_inc(fill_set, 1)
            nc.gpsimd.memset(ones_c[:, :], 1.0)
            nc.gpsimd.memset(ones_m[:, :], 1.0)
            nc.gpsimd.memset(mask_a[:, 0:DH], 1.0)
            nc.gpsimd.memset(mask_a[:, DH:P], 0.0)
            nc.gpsimd.memset(mask_b[:, 0:DH], 0.0)
            nc.gpsimd.memset(mask_b[:, DH:P], 1.0)
            link(nc.gpsimd.memset(head_ones[:, :], 0.0))
            link(nc.gpsimd.memset(head_ones[0:DH, 0:DH], 1.0))
            link(nc.gpsimd.memset(head_ones[DH:P, DH:P], 1.0))
            nc.gpsimd.memset(ident[:, :], 0.0)
            link(nc.gpsimd.memset(before[:, :], 1.0))
            nc.gpsimd.affine_select(out=ident[:, :], in_=ident[:, :], compare_op=ALU.not_equal, fill=1.0,
                                    base=0, pattern=[[-1, P]], channel_multiplier=1)
            nc.gpsimd.affine_select(out=before[:, :], in_=before[:, :], compare_op=ALU.is_gt, fill=0.0,
                                    base=0, pattern=[[1, P]], channel_multiplier=-1)
            nc.gpsimd.iota(iota_f[:, :], pattern=[[1, P]], base=0, channel_multiplier=0,
                           allow_small_or_imprecise_dtypes=True)
            nc.gpsimd.iota(iota_d[:, :], pattern=[[1, P]], base=0, channel_multiplier=0,
                           allow_small_or_imprecise_dtypes=True)
            nc.gpsimd.iota(iota_s[:, :], pattern=[[1, TP]], base=-1, channel_multiplier=0,
                           allow_small_or_imprecise_dtypes=True).then_inc(const_done, 1)
            gp.wait_ge(fill_out, 64)
            gp.wait_ge(scat_ready, 1)
            for c in range(EC):
                nc.gpsimd.indirect_dma_start(
                    out=e_dram, out_offset=bass.IndirectOffsetOnAxis(ap=pos_i[:, c:c + 1], axis=0),
                    in_=pairs[:, c, :], in_offset=None).then_inc(scat_done, 16)
            gp.wait_ge(edges_placed, 1)
            gp.wait_ge(h1_done, NB)
            gp.wait_ge(ks_ps, 1)
            gp.wait_ge(qk_out[0], 32 * NPAIR)
            gp.wait_ge(qk_out[1], 32 * NPAIR)
            nc.gpsimd.memset(ACC[:, NB - 1, :], 0.0).then_inc(x_pad, 1)
            gp.wait_ge(x_pad, 2)
            gp.dma_start(ACC[:, 0:NB - 1, :], x[0:(NB - 1) * P, :].rearrange("(b p) d -> p b d", p=P)).then_inc(xr_in, 16)
            gp.dma_start(ACC[0:LAST, NB - 1, :], x[(NB - 1) * P:T, :]).then_inc(xr_in, 16)
            gp.dma_start(bo_all[:, :], row_bcast(bo)).then_inc(xr_in, 16)
            gp.dma_start(WO_RAW[:, :, :], w_view(WoT)).then_inc(wo_in, 16)
            link(nc.gpsimd.memset(head_rows[:, :], 1.0))
            link(nc.gpsimd.affine_select(out=head_rows[:, :], in_=head_rows[:, :], compare_op=ALU.is_ge, fill=0.0,
                                         base=0, pattern=[[1, D]], channel_multiplier=-DH))
            nc.gpsimd.affine_select(out=head_rows[:, :], in_=head_rows[:, :], compare_op=ALU.is_ge, fill=0.0,
                                    base=DH - 1, pattern=[[-1, D]], channel_multiplier=DH).then_inc(head_rows_done, 1)
            gp.wait_ge(xr_in, 48)
            nc.gpsimd.tensor_tensor(ACC[:, :, :], ACC[:, :, :], bo_all[:, None, :].to_broadcast([P, NB, D]),
                                    ALU.add).then_inc(xr_b, 1)
            for p in range(NPAIR - 1):
                gp.wait_ge(o_out, NB * (p + 1))
                nc.gpsimd.tensor_tensor(OP[:, p, :], OP[:, p, :], OM[:, p, :], ALU.add).then_inc(o_sum, 1)
            gp.wait_ge(wo_lo, 1)
            gp.wait_ge(xr_b, 1)
            nc.gpsimd.memset(CT[:, 7:NB, :], 2.0)
            gp.wait_ge(o_sum, NPAIR)
            nc.gpsimd.memset(CT[:, 3:7, :], 2.0)
            gp.wait_ge(on_lo, NPAIR * NT)
            link(nc.gpsimd.memset(CT[:, 0:3, :], 2.0))
            for b in range(NB):
                nc.gpsimd.affine_select(out=CT[:, b, 0:CW], in_=CT[:, b, 0:CW], compare_op=ALU.is_ge, fill=0.0,
                                        base=-1 - b * P, pattern=[[1, CW]], channel_multiplier=-1).then_inc(ct_add, 1)
            gp.wait_ge(e_ready, 1)
            for i in range(NSC):
                if i >= 2:
                    gp.wait_ge(ct_ps, i - 1)
                for j in range(4):
                    nc.gpsimd.tensor_scalar(OHD[i % 2][:, j, :], iota_d[:, :], e_df[:, 4 * i + j:4 * i + j + 1], None,
                                            ALU.is_equal).then_inc(oh_pool, 1)

        def one(ap3):
            return ap3.rearrange("p a d -> p (a d)")

        @block.scalar
        def _(act):
            def xt_high(b):
                act.wait_ge(xt_ps, b + 1)
                nc.scalar.activation(XT[0][:, :, bass.ds(b * P, P)],
                                     PS[:, bass.ds(b % 2, 1), :].rearrange("p a (c t) -> p (a c) t", c=KC),
                                     ACT.Copy).then_inc(xt_hi, 1)

            def v_high(b):
                act.wait_ge(v_biased, b + 1)
                nc.scalar.activation(VV[:, :, bass.ds(b, 1), 0:DH].rearrange("p h a d -> p (h a) d"),
                                     vt[:, bass.ds(b % 2, 1), :].rearrange("p a (h d) -> p (a h) d", h=H),
                                     ACT.Copy).then_inc(v_hi, 1)

            xt_high(0)
            xt_high(1)
            for n in range(2):
                act.wait_ge(w_in[n], 16)
                nc.scalar.activation(WH[n][0][:, :, :], WRAW[n][:, :, :], ACT.Copy).then_inc(w_hi, 1)
            with act.Fori(0, NB - 2) as b:
                v_high(b)
                xt_high(b + 2)
            v_high(NB - 2)
            v_high(NB - 1)
            for n in range(2):
                act.wait_ge(w_in[n + 2], 16)
                act.wait_ge((v_ps, h1_ps)[n], NB)
                nc.scalar.activation(WH[n][0][:, :, :], WRAW[n][:, :, :], ACT.Copy).then_inc(w_hi, 1)
            act.wait_ge(bias_in, 16 * 7)
            act.wait_ge(xn_ready, NB)
            act.wait_ge(xt_ps, NB)
            for j in range(2 * NPAIR):
                pr = j % NPAIR
                bias = (bq_sb if j < NPAIR else bk_sb)[:, pr:pr + 1]
                if j >= 2:
                    act.wait_ge(qk_out[j % 2], 32 * (j // 2))
                if j >= NPAIR + 2:
                    act.wait_ge(ks_read, j - NPAIR - 1)
                for t, (c0, w) in enumerate(TILES):
                    n = NT * j + t
                    act.wait_ge(qk_ps, n + 1)
                    nc.scalar.activation(QF[j % 2][:, c0:c0 + w], PS[:, n % 4, 0:w], ACT.Relu, bias=bias)
                    nc.scalar.activation(QH[j % 2][:, c0:c0 + w], PS[:, n % 4, 0:w], ACT.Relu,
                                         bias=bias).then_inc(qk_act, 1)

            def exp_step(p, i):
                g = p * (2 * NB) + i
                act.wait_ge(s_neg, g + 1)
                if not (first(p) and i < 2):
                    act.wait_ge(pt_ps, g * 2 - 2)
                nc.scalar.activation(PR[i % 2][:, 0:T], SN[i % 2][:, :], ACT.Exp, scale=-1.0,
                                     bias=negmax[:, i % 2:i % 2 + 1],
                                     accum_out=rowsum[:, bass.ds(g, 1)]).then_inc(p_exp, 1)

            def hi_step(p, i):
                g = p * (2 * NB) + i
                if i % 2 == 0 and not (first(p) and i < 4):
                    act.wait_ge(av_done, p * NB + i // 2 - 1)
                for part, (b0, b1) in enumerate(PARTS):
                    act.wait_ge(pt_ps, g * 2 + (part + 1))
                    nc.scalar.activation(PT[i // 2 % 2][0][:, b0:b1, (i % 2) * P:(i % 2 + 1) * P], pt_banks(b0, b1),
                                         ACT.Copy).then_inc(pt_hi, 1)

            def out_step(p, k):
                a, m = ((OP, OM) if k < NB // 2 else (OM, OP))
                cols = slice((k % (NB // 2)) * 2 * P, (k % (NB // 2) + 1) * 2 * P)
                act.wait_ge(av_done, p * NB + k + 1)
                keep, move = ((slice(0, DH), slice(DH, P)) if k < NB // 2 else (slice(DH, P), slice(0, DH)))
                nc.scalar.activation(one(OP[keep, bass.ds(p, 1), cols]), PS[keep, 6 + k % 2, 0:2 * P], ACT.Copy)
                nc.scalar.activation(one(OM[keep, bass.ds(p, 1), cols]), PS[move, 6 + k % 2, 0:2 * P],
                                     ACT.Copy).then_inc(o_out, 1)

            def first(p):
                return type(p) is int and p == 0

            def att_steps(p):
                for i in range(2 * NB):
                    if i > 0:
                        hi_step(p, i - 1)
                    elif not first(p):
                        hi_step(p - 1, 2 * NB - 1)
                    exp_step(p, i)
                    if i % 2 == 1:
                        k = (i - 5) // 2
                        if first(p) and k == 0:
                            for r in range(2):
                                act.wait_ge(qk_out[r], 32 * NPAIR)
                        if k >= 0:
                            out_step(p, k)
                        elif not first(p):
                            out_step(p - 1, k + NB)

            att_steps(0)
            with act.Fori(1, NPAIR) as p:
                att_steps(p)
            hi_step(NPAIR - 1, 2 * NB - 1)
            for k in range(NB - 2, NB):
                out_step(NPAIR - 1, k)

            act.wait_ge(wo_in, 16)
            nc.scalar.activation(WO[0][:, :, :], WO_RAW[:, :, :], ACT.Copy).then_inc(wo_hi, 1)
            act.wait_ge(rt_ps, 1)
            nc.scalar.activation(sums_t[:, :], ps_flat[0:H, 3 * 512:3 * 512 + TP], ACT.Copy).then_inc(rt_done, 1)
            act.wait_ge(av_done, NG // 2)
            for t, (c0, w) in enumerate(TILES):
                for p in range(NPAIR):
                    act.wait_ge(on_f, NPAIR * t + p + 1)
                    nc.scalar.activation(ON[0][:, p, c0:c0 + w], OP[:, p, c0:c0 + w], ACT.Copy).then_inc(on_hi, 1)

            def steps_up(i, par, wait=True):
                if wait:
                    act.wait_ge(ct_ps, i - 1)
                for j in (2, 3):
                    nc.scalar.activation(OHS[4 * par + j][:, 0:CW], iota_s[:, 0:CW], ACT.Sign,
                                         bias=e_half[:, bass.ds(i * 4 + j, 1)]).then_inc(oh_act, 1)

            act.wait_ge(e_ready, 1)
            steps_up(0, 0, wait=False)
            steps_up(1, 1, wait=False)
            act.wait_ge(w2_in, 32)
            nc.scalar.activation(W2H[0][:, :, :], W2_RAW[:, :, :], ACT.Copy).then_inc(w2_hi, 1)
            with act.Fori(1, NSC // 2) as k:
                steps_up(k * 2, 0)
                steps_up(k * 2 + 1, 1)
            act.wait_ge(ct_add, NB + NSC)
            act.wait_ge(dd_ready, 1)
            for b in range(NB):
                nc.scalar.activation(HS[0][:, b, :], H1[:, b, :], ACT.Copy, scale=dinv[:, b:b + 1]).then_inc(hs_hi, 1)
                if b == 0:
                    act.wait_ge(rt_ps, 2)
                    nc.scalar.activation(roots_t[:, :], ps_flat[0:1, 5 * 512:5 * 512 + TP], ACT.Copy).then_inc(rt_done, 1)
                if 2 <= b < 2 + NT:
                    c0, w = TILES[b - 2]
                    act.wait_ge(dr_ps, b - 1)
                    nc.scalar.activation(dinv_all[:, c0:c0 + w], PS[:, 6 + (b - 2) % 2, 0:w], ACT.Copy).then_inc(dr_done, 1)
            act.wait_ge(hs_lo, NB)
            for c in range(KC):
                act.wait_ge(bn_done, max(c, 1))
                scale, bias = small[:, c:c + 1], small[:, KC + c:KC + c + 1]
                nc.scalar.activation(GR[0][:, c, :], G[:, c, :], ACT.Relu, scale=scale, bias=bias)
                nc.scalar.activation(G[:, c, :], G[:, c, :], ACT.Relu, scale=scale, bias=bias).then_inc(gr_relu, 1)
            act.wait_ge(g_ps, KC * NT)
            with act.Fori(0, NB) as b:
                act.wait_ge(h2_b, b + 1)
                nc.scalar.activation(one(H2[0][:, bass.ds(b, 1), :]), one(ht[:, bass.ds(b % 2, 1), :]), ACT.Copy,
                                     scale=dinv[:, bass.ds(b, 1)]).then_inc(h2_hi, 1)

            act.wait_ge(f_in, 64)
            for raw, hi in ((RW_RAW, RW[0]), (F1_RAW, F1[0]), (F2_RAW, F2[0])):
                nc.scalar.activation(hi[:, :, :], raw[:, :, :], ACT.Copy).then_inc(f_hi, 1)
            nc.scalar.activation(ones_r[:, :], ones_m[0:1, :], ACT.Copy)
            act.wait_ge(f_lo, 3)
            nc.scalar.activation(FB2[0][:, :], fb2_row[:, :], ACT.Copy).then_inc(f_hi, 1)

            def x2t_high(b):
                act.wait_ge(x2t_ps, b + 1)
                nc.scalar.activation(X2T[0][:, :, blk(b)], PS[:, 2 + b % 2, :].rearrange("p (c t) -> p c t", c=KC),
                                     ACT.Copy).then_inc(x2t_hi, 1)

            def gelu(t, f):
                n, (c0, w) = FC * t + f, TILES[t]
                act.wait_ge(u_ps, n + 1)
                nc.scalar.activation(HF[:, f, c0:c0 + w], PS[:, (6, 7, 0)[n % 3], 0:w], ACT.Gelu,
                                     bias=fb1_sb[:, f:f + 1]).then_inc(u_gelu, 1)
                act.wait_ge(u_gelu, n + 1)
                nc.scalar.activation(HFH[0][:, f, c0:c0 + w], HF[:, f, c0:c0 + w], ACT.Copy).then_inc(u_hi, 1)

            for b in range(8):
                x2t_high(b)
            act.wait_ge(a2_ps, NB)
            gelu(0, 0)
            gelu(0, 1)
            x2t_high(8)
            x2t_high(9)
            for t in (1, 2):
                for f in range(FC):
                    gelu(t, f)
            act.wait_ge(mk_done, 2)
            for b in range(NB):
                nc.scalar.activation(EL[:, b, :], LG[:, b, :], ACT.Exp, bias=l1neg[:, b:b + 1],
                                     accum_out=zsum[:, b:b + 1]).then_inc(el_done, 1)

        @block.vector
        def _(ve):
            V = nc.vector
            link = Chain(ve, dve)

            def rsqrt(out_t, in_t, n):
                t, ti = nt_a[:, 0:n], nt_i[:, 0:n]
                link(V.tensor_scalar(ti, in_t.bitcast(I32), 1, None, ALU.logical_shift_right))
                link(V.tensor_scalar(out_t.bitcast(I32), ti, float(-0x5F3759DF), -1.0, ALU.add, ALU.mult))
                for _ in range(3):
                    link(V.scalar_tensor_tensor(t, out_t, -0.5, out_t, ALU.mult, ALU.mult))
                    link(V.tensor_tensor(t, t, in_t, ALU.mult))
                    link(V.scalar_tensor_tensor(out_t, t, 1.5, out_t, ALU.add, ALU.mult))

            def layernorm(b0, b1, src_of, dst_of, free, arrived, done):
                for b in range(b0, b1):
                    arrived(b)
                    last = V.bn_stats(ln_st[:, b, :], src_of(b))
                link(last)
                for b in range(b0, b1):
                    last = V.bn_aggr(ln_mv[:, b, :], ln_st[:, b, :])
                link(last)
                link(V.tensor_scalar(var_c[:, b0:b1], ln_mv[:, b0:b1, 1], EPS_LN, None, ALU.add))
                rsqrt(rstd[:, b0:b1], var_c[:, b0:b1], b1 - b0)
                for b in range(b0, b1):
                    free(b)
                    V.tensor_scalar(dst_of(b), src_of(b), ln_mv[:, b, 0:1], rstd[:, b:b + 1],
                                    ALU.subtract, ALU.mult).then_inc(done, 1)

            def layernorm_1(b0, b1):
                layernorm(b0, b1, lambda b: X[:, b, :], lambda b: X[:, b, :], lambda b: None,
                          lambda b: ve.wait_ge(x_in[b], 16), xn_ready)

            layernorm_1(0, 2)
            layernorm_1(2, 6)

            def weight_low(n):
                ve.wait_ge(w_hi, n + 1)
                V.tensor_tensor(WH[n % 2][1][:, :, :], WRAW[n % 2][:, :, :], WH[n % 2][0][:, :, :].bitcast(F32),
                                ALU.subtract).then_inc(w_lo, 1)

            def xt_low(b):
                ve.wait_ge(xt_hi, b + 1)
                V.tensor_tensor(XT[1][:, :, bass.ds(b * P, P)],
                                PS[:, bass.ds(b % 2, 1), :].rearrange("p a (c t) -> p (a c) t", c=KC),
                                XT[0][:, :, bass.ds(b * P, P)].bitcast(F32), ALU.subtract).then_inc(xt_lo, 1)

            def v_bias(b):
                ve.wait_ge(v_ps, b + 1)
                V.tensor_tensor(one(vt[:, bass.ds(b % 2, 1), :]), one(PS[:, bass.ds(b % 2 + 2, 1), :]), bv_all[:, :],
                                ALU.add).then_inc(v_biased, 1)

            def h1_bias(b):
                ve.wait_ge(h1_ps, b + 1)
                V.tensor_tensor(one(H1[:, bass.ds(b, 1), :]), one(PS[:, bass.ds(b % 2 + 4, 1), :]), b1_all[:, :],
                                ALU.add).then_inc(h1_done, 1)

            def v_low(b):
                ve.wait_ge(v_hi, b + 1)
                V.tensor_tensor(VV[:, :, bass.ds(b, 1), DH:P].rearrange("p h a d -> p (h a) d"),
                                vt[:, bass.ds(b % 2, 1), :].rearrange("p a (h d) -> p (a h) d", h=H),
                                VV[:, :, bass.ds(b, 1), 0:DH].rearrange("p h a d -> p (h a) d").bitcast(F32),
                                ALU.subtract).then_inc(v_lo, 1)

            xt_low(0)
            xt_low(1)
            weight_low(0)
            weight_low(1)
            layernorm_1(6, NB)

            ve.wait_ge(edge_in, 32)
            ve.wait_ge(const_done, 1)
            link(V.tensor_scalar(e_bkt[:, :], e_dst[:, :], 7, None, ALU.logical_shift_right))
            link(V.tensor_copy(e_bf[:, :], e_bkt[:, :]))

            def bucket_total(b):
                V.tensor_scalar(e_mask[:, :], e_bf[:, :], iota_f[0:EP, b:b + 1], None, ALU.is_equal, ALU.add,
                                accum_out=e_tot[0:EP, b:b + 1]).then_inc(etot_ready, 1)

            ve.wait_ge(bias_in, 16 * 7)
            for b in range(2):
                v_bias(b)
                h1_bias(b)
                v_low(b)
                xt_low(b + 2)
                for e in range(b * NB // 2, (b + 1) * NB // 2):
                    if e > 0:
                        ve.wait_ge(etot_ready, e)
                    bucket_total(e)
            with ve.Fori(2, NB - 2) as b:
                ve.wait_ge(v_lo, b - 1)
                v_bias(b)
                h1_bias(b)
                v_low(b)
                xt_low(b + 2)
            ve.wait_ge(v_lo, NB - 3)
            v_bias(NB - 2)
            h1_bias(NB - 2)
            v_low(NB - 2)
            ve.wait_ge(v_lo, NB - 2)
            v_bias(NB - 1)
            weight_low(2)
            h1_bias(NB - 1)
            v_low(NB - 1)
            weight_low(3)

            def edge_offsets():
                ve.wait_ge(epre_ready, 1)
                link(V.tensor_copy(e_cnti[:, :], PS[:, 7, 64:64 + NB]))
                link(V.tensor_scalar(e_cnt[:, :], e_cnti[:, :], float(SC - 1), None, ALU.add))
                link(V.tensor_copy(e_cnti[:, :], e_cnt[:, :]))
                link(V.tensor_scalar(e_cnti[:, :], e_cnti[:, :], 9, None, ALU.logical_shift_right))
                link(V.tensor_copy(e_nsc[:, :], e_cnti[:, :]))
                link(V.tensor_tensor_scan(e_end[:, :], ones_c[:, 0:NB], e_nsc[:, :], 0.0, ALU.mult, ALU.add))
                link(V.tensor_tensor(e_base[:, :], e_end[:, :], e_nsc[:, :], ALU.subtract))
                link(V.tensor_scalar(e_base[:, :], e_base[:, :], float(SC), -1.0, ALU.mult, ALU.add))
                link(V.tensor_tensor(e_base[:, :], PS[:, 7, 0:NB], e_base[:, :], ALU.add))
                link(V.memset(e_pos[:, :], 0.0))

            def edge_bucket(b):
                link(V.tensor_scalar(e_mask[:, :], e_bf[:, :], iota_f[0:EP, b:b + 1], None, ALU.is_equal))
                link(V.tensor_tensor_scan(e_cum[:, :], ones_c[0:EP, 0:EC], e_mask[:, :], 0.0, ALU.mult, ALU.add))
                link(V.scalar_tensor_tensor(e_cum[:, :], e_cum[:, :], e_base[0:EP, b:b + 1], e_mask[:, :],
                                            ALU.add, ALU.mult))
                link(V.tensor_tensor(e_pos[:, :], e_pos[:, :], e_cum[:, :], ALU.add))

            def edge_places():
                link(V.tensor_copy(e_tmp[:, :], e_pos[:, :]))
                link(V.tensor_scalar(pos_i[:, :], e_tmp[:, :], 2, P - 1, ALU.logical_shift_right, ALU.bitwise_and))
                link(V.tensor_scalar(pos_i[:, :], pos_i[:, :], float(NCH), None, ALU.mult))
                link(V.tensor_scalar(e_bkt[:, :], e_tmp[:, :], 9, 2, ALU.logical_shift_right, ALU.logical_shift_left))
                link(V.tensor_tensor(pos_i[:, :], pos_i[:, :], e_bkt[:, :], ALU.add))
                link(V.tensor_scalar(e_tmp[:, :], e_tmp[:, :], 3, None, ALU.bitwise_and))
                link(V.tensor_tensor(pos_i[:, :], pos_i[:, :], e_tmp[:, :], ALU.add))
                link(V.tensor_scalar(pairs[:, :, 0], e_dst[:, :], P - 1, None, ALU.bitwise_and))
                V.tensor_copy(pairs[:, :, 1], e_src[:, :]).then_inc(scat_ready, 1)

            def superchunk_offsets():
                link(V.memset(e_acc[:, :], 0.0))
                for b in range(NB):
                    link(V.scalar_tensor_tensor(e_acc[:, :], iota_f[0:1, 0:NSC], e_end[0:1, b:b + 1], e_acc[:, :],
                                                ALU.is_ge, ALU.add))
                link(V.tensor_scalar(e_acc[:, :], e_acc[:, :], float(NB - 1), float(TP), ALU.min, ALU.mult))
                V.tensor_copy(bkt_row[:, :], e_acc[:, :]).then_inc(edges_placed, 1)
                ve.wait_ge(edges_placed, 1)

            EDGE_J = (NB + 1) // 2
            for j in range(2 * NPAIR):
                f, hi, lo = QF[j % 2], QH[j % 2], QL[j % 2]
                for t, (c0, w) in enumerate(TILES):
                    n, c = NT * j + t, slice(c0, c0 + w)
                    ve.wait_ge(qk_act, n + 1)
                    V.tensor_tensor(lo[:, c], f[:, c], hi[:, c].bitcast(F32), ALU.subtract).then_inc(qk_lo, 1)
                if j == 0:
                    edge_offsets()
                if j < EDGE_J:
                    for b in range(2 * j, min(2 * j + 2, NB)):
                        edge_bucket(b)
                elif j == EDGE_J:
                    edge_places()
                elif j == EDGE_J + 1:
                    superchunk_offsets()

            ve.wait_ge(ks_ps, 1)
            link(V.tensor_scalar(negr[:, :], PS[:, 6, 0:NG], EPS_K, None, ALU.add))
            link(V.reciprocal(negr[:, :], negr[:, :]))
            link(V.tensor_scalar(negr[:, :], negr[:, :], -1.0, None, ALU.mult))

            def first(p):
                return type(p) is int and p == 0

            def neg_step(p, i):
                g = p * (2 * NB) + i
                ve.wait_ge(s_ready, g + 1)
                if not (first(p) and i < 2):
                    ve.wait_ge(p_exp, g - 1)
                V.tensor_scalar(SN[i % 2][:, :], ps_flat[:, 0:T], negr[:, bass.ds(g, 1)], None, ALU.mult, ALU.min,
                                accum_out=negmax[:, i % 2:i % 2 + 1]).then_inc(s_neg, 1)

            def lo_step(p, i):
                g = p * (2 * NB) + i
                q = slice((i % 2) * P, (i % 2 + 1) * P)
                for part, (b0, b1) in enumerate(PARTS):
                    ve.wait_ge(pt_hi, g * 2 + (part + 1))
                    V.tensor_tensor(PT[i // 2 % 2][1][:, b0:b1, q], pt_banks(b0, b1),
                                    PT[i // 2 % 2][0][:, b0:b1, q].bitcast(F32), ALU.subtract).then_inc(pt_lo, 1)

            def att_steps(p):
                for i in range(2 * NB):
                    neg_step(p, i)
                    if i > 0:
                        lo_step(p, i - 1)
                    elif not first(p):
                        lo_step(p - 1, 2 * NB - 1)

            ve.wait_ge(ks_ps, 1)
            for s in range(2):
                V.memset(PR[s][:, T:TP], 0.0).then_inc(p_pad, 1)
            att_steps(0)
            with ve.Fori(1, NPAIR) as p:
                att_steps(p)
            lo_step(NPAIR - 1, 2 * NB - 1)

            ve.wait_ge(p_exp, NG)
            V.reciprocal(rowsum[:, :], rowsum[:, :]).then_inc(rinv_done, 1)
            ve.wait_ge(o_out, NG // 2)
            V.tensor_tensor(OP[:, NPAIR - 1, :], OP[:, NPAIR - 1, :], OM[:, NPAIR - 1, :], ALU.add).then_inc(o_sum, 1)
            ve.wait_ge(o_sum, NPAIR)

            def normalise(t, p):
                n, (c0, w) = NPAIR * t + p, TILES[t]
                ve.wait_ge(r_ps, n + 1)
                V.tensor_tensor(OP[:, p, c0:c0 + w], PS[:, n % 3, 0:w], OP[:, p, c0:c0 + w], ALU.mult).then_inc(on_f, 1)

            def normal_low(t, p):
                n, (c0, w) = NPAIR * t + p, TILES[t]
                ve.wait_ge(on_hi, n + 1)
                V.tensor_tensor(ON[1][:, p, c0:c0 + w], OP[:, p, c0:c0 + w], ON[0][:, p, c0:c0 + w].bitcast(F32),
                                ALU.subtract).then_inc(on_lo, 1)

            steps = [(t, p) for t in range(NT) for p in range(NPAIR)]
            for n, (t, p) in enumerate(steps):
                normalise(t, p)
                if n == 1:
                    ve.wait_ge(wo_hi, 1)
                    V.tensor_tensor(WO[1][:, :, :], WO_RAW[:, :, :], WO[0][:, :, :].bitcast(F32),
                                    ALU.subtract).then_inc(wo_lo, 1)
                if n > 0:
                    normal_low(*steps[n - 1])
            normal_low(*steps[-1])

            def acc_add(b):
                ve.wait_ge(wo_ps, b + 1)
                V.tensor_tensor(one(ACC[:, bass.ds(b, 1), :]), one(PS[:, bass.ds(b % 4 + 4, 1), :]),
                                one(ACC[:, bass.ds(b, 1), :]), ALU.add).then_inc(acc_done, 1)

            ve.wait_ge(xr_b, 1)
            for b in range(4):
                acc_add(b)
            ve.wait_ge(edges_back, 16)
            V.tensor_copy(e_df[:, :], e_load[:, :, 0])
            link(V.tensor_copy(e_sf[:, :], e_load[:, :, 1]))
            V.tensor_scalar(e_half[:, :], e_sf[:, :], -1.0, 0.5, ALU.mult, ALU.add).then_inc(e_ready, 1)
            ve.wait_ge(e_ready, 1)
            ve.wait_ge(r_ps, NPAIR * NT)
            ct_flat = CT[:, :, :].rearrange("p b t -> p (b t)")

            def step_rows(i, par, wait=True):
                if wait:
                    ve.wait_ge(ct_ps, i - 1)
                for j in range(2):
                    V.tensor_scalar(OHS[4 * par + j][:, 0:CW], iota_s[:, 0:CW], e_sf[:, bass.ds(i * 4 + j, 1)], 2.0,
                                    ALU.is_ge, ALU.mult).then_inc(oh_dve, 1)

            def add_counts(i, par):
                off = ve.value_load(bkt_row[0:1, bass.ds(i, 1)], min_val=0, max_val=(NB - 1) * TP)
                ve.wait_ge(ct_ps, i + 1)
                ve.wait_ge(ct_add, i + NB)
                V.tensor_tensor(ct_flat[:, bass.ds(off, CW)], ps_flat[:, par * 2048:par * 2048 + CW],
                                ct_flat[:, bass.ds(off, CW)], ALU.add).then_inc(ct_add, 1)

            step_rows(0, 0, wait=False)
            step_rows(1, 1, wait=False)
            with ve.Fori(4, NB) as b:
                acc_add(b)

            ve.wait_ge(ct_add, NB)
            add_counts(0, 0)
            step_rows(2, 0)
            add_counts(1, 1)
            with ve.Fori(1, NSC // 2 - 1) as k:
                step_rows(k * 2 + 1, 1)
                add_counts(k * 2, 0)
                step_rows(k * 2 + 2, 0)
                add_counts(k * 2 + 1, 1)
            step_rows(NSC - 1, 1)
            add_counts(NSC - 2, 0)
            add_counts(NSC - 1, 1)
            ve.wait_ge(ct_add, NB + NSC)
            link(V.tensor_tensor(deg[:, :], CT[:, :, T], CT[:, :, 0], ALU.subtract))
            V.tensor_scalar(deg[:, :], deg[:, :], 0.5, 1.0, ALU.mult, ALU.max).then_inc(deg_done, 1)
            ve.wait_ge(deg_done, 1)
            rsqrt(dinv[:, :], deg[:, :], NB)
            V.tensor_scalar(dinv_half[:, :], dinv[:, :], 0.5, None, ALU.mult).then_inc(dd_ready, 1)

            for b in range(NB):
                link(V.tensor_tensor(CTR[:, b, 0:TP - 1], CT[:, b, 1:TP], CT[:, b, 0:TP - 1], ALU.subtract))
                V.tensor_scalar(CTR[:, b, TP - 1:TP], CT[:, b, TP - 1:TP], 0.0, None, ALU.mult).then_inc(ct_ready, 1)
                ve.wait_ge(hs_hi, b + 1)
                V.scalar_tensor_tensor(HS[1][:, b, :], H1[:, b, :], dinv[:, b:b + 1], HS[0][:, b, :].bitcast(F32),
                                       ALU.mult, ALU.subtract).then_inc(hs_lo, 1)
            ve.wait_ge(w2_hi, 1)
            V.tensor_tensor(W2H[1][:, :, :], W2_RAW[:, :, :], W2H[0][:, :, :].bitcast(F32), ALU.subtract).then_inc(w2_lo, 1)
            ve.wait_ge(dr_done, NT)

            def channel_stats(c):
                for t, (c0, w) in enumerate(TILES):
                    n = NT * c + t
                    ve.wait_ge(g_ps, n + 1)
                    V.tensor_tensor(G[:, c, c0:c0 + w], PS[:, n % 8, 0:w], dinv_all[:, c0:c0 + w],
                                    ALU.mult).then_inc(g_done, 1)
                ve.wait_ge(g_done, NT * (c + 1))
                for t, (c0, w) in enumerate(KTILES):
                    last = V.bn_stats(ln_st[:, t, :], G[:, c, c0:c0 + w])
                link(last)
                link(V.bn_aggr(ln_mv[:, c, :], ln_st[:, 0:NT, :]))

            def batch_norm(c0, c1):
                c, cb = slice(c0, c1), slice(KC + c0, KC + c1)
                link(V.tensor_scalar(var_c[:, c], ln_mv[:, c, 1], EPS_LN, None, ALU.add))
                rsqrt(rstd[:, c], var_c[:, c], c1 - c0)
                link(V.tensor_tensor(small[:, c], gamma_sb[:, c], rstd[:, c], ALU.mult))
                link(V.tensor_tensor(small[:, cb], ln_mv[:, c, 0], small[:, c], ALU.mult))
                V.tensor_tensor(small[:, cb], beta_sb[:, c], small[:, cb], ALU.subtract).then_inc(bn_done, 1)

            def relu_low(c):
                ve.wait_ge(gr_relu, c + 1)
                V.tensor_tensor(GR[1][:, c, :], G[:, c, :], GR[0][:, c, :].bitcast(F32), ALU.subtract).then_inc(gr_lo, 1)

            channel_stats(0)
            channel_stats(1)
            batch_norm(0, 2)
            channel_stats(2)
            relu_low(0)
            relu_low(1)
            batch_norm(2, 3)
            channel_stats(3)
            relu_low(2)
            batch_norm(3, 4)
            relu_low(3)

            def h2_bias(b):
                ve.wait_ge(h2_ps, b + 1)
                V.tensor_tensor(one(ht[:, bass.ds(b % 2, 1), :]), one(PS[:, bass.ds((b + 4) % 8, 1), :]), b2_all[:, :],
                                ALU.add).then_inc(h2_b, 1)

            def h2_low(b):
                ve.wait_ge(h2_hi, b + 1)
                V.scalar_tensor_tensor(one(H2[1][:, bass.ds(b, 1), :]), one(ht[:, bass.ds(b % 2, 1), :]),
                                       dinv[:, bass.ds(b, 1)], one(H2[0][:, bass.ds(b, 1), :]).bitcast(F32),
                                       ALU.mult, ALU.subtract).then_inc(h2_lo, 1)

            h2_bias(0)
            h2_bias(1)
            h2_low(0)
            with ve.Fori(2, NB) as b:
                ve.wait_ge(h2_lo, b - 1)
                h2_bias(b)
                h2_low(b - 1)
            h2_low(NB - 1)

            for n, (raw, (hi, lo)) in enumerate(((RW_RAW, RW), (F1_RAW, F1), (F2_RAW, F2))):
                ve.wait_ge(f_hi, n + 1)
                V.tensor_tensor(lo[:, :, :], raw[:, :, :], hi[:, :, :].bitcast(F32), ALU.subtract).then_inc(f_lo, 1)
            ve.wait_ge(f_hi, 4)
            V.tensor_tensor(FB2[1][:, :], fb2_row[:, :], FB2[0][:, :].bitcast(F32), ALU.subtract).then_inc(f_lo, 1)

            def x2_add(b):
                ve.wait_ge(a2_ps, b + 1)
                V.scalar_tensor_tensor(ACC[:, b, :], PS[:, (6, 7, 0, 1)[b % 4], :], dinv_half[:, b:b + 1], ACC[:, b, :],
                                       ALU.mult, ALU.add).then_inc(x2_done, 1)

            def x2t_low(b):
                ve.wait_ge(x2t_hi, b + 1)
                V.tensor_tensor(X2T[1][:, :, blk(b)], PS[:, 2 + b % 2, :].rearrange("p (c t) -> p c t", c=KC),
                                X2T[0][:, :, blk(b)].bitcast(F32), ALU.subtract).then_inc(x2t_lo, 1)

            def layernorm_2(b0, b1):
                layernorm(b0, b1, lambda b: ACC[:, b, :], lambda b: XN[b % 4][:, :],
                          lambda b: ve.wait_ge(x2t_ps, b - 3) if b >= 4 else None,
                          lambda b: ve.wait_ge(x2_done, b + 1), xn2_ready)

            def hidden_low(t):
                c0, w = TILES[t]
                for f in range(FC):
                    ve.wait_ge(u_hi, FC * t + f + 1)
                    V.tensor_tensor(HFH[1][:, f, c0:c0 + w], HF[:, f, c0:c0 + w], HFH[0][:, f, c0:c0 + w].bitcast(F32),
                                    ALU.subtract).then_inc(u_lo, 1)

            ve.wait_ge(f_lo, 4)
            for b in range(4):
                x2_add(b)
            layernorm_2(0, 4)
            x2_add(4)
            x2_add(5)
            x2t_low(0)
            x2t_low(1)
            x2_add(6)
            x2t_low(2)
            x2t_low(3)
            x2_add(7)
            layernorm_2(4, 8)
            x2_add(8)
            x2_add(9)
            layernorm_2(8, NB)
            for b in range(4, NB):
                x2t_low(b)
            hidden_low(0)
            cols = iota_f[:, None, 0:NE]

            def route(b0, b1, bank):
                n = b1 - b0
                ve.wait_ge(lg_ps, b1)
                link(V.tensor_copy(LG[:, b0:b1, :], PS[:, bank, 0:n * NE].rearrange("p (b e) -> p b e", e=NE)))
                for b in range(b0, b1):
                    last = V.max(top8[:, b, :], LG[:, b, :])
                link(last)
                for b in range(b0, b1):
                    last = V.max_index(idx8[:, b, :], top8[:, b, :], LG[:, b, :])
                link(last)
                V.tensor_scalar(l1neg[:, b0:b1], top8[:, b0:b1, 0], -1.0, None, ALU.mult)
                link(V.tensor_copy(idxf[:, b0:b1, :], idx8[:, b0:b1, :]))
                V.tensor_tensor(MK[:, b0:b1, :], cols.to_broadcast([P, n, NE]),
                                idxf[:, b0:b1, 0:1].to_broadcast([P, n, NE]), ALU.is_equal)
                link(V.tensor_tensor(EL[:, b0:b1, :], cols.to_broadcast([P, n, NE]),
                                     idxf[:, b0:b1, 1:2].to_broadcast([P, n, NE]), ALU.is_equal))
                link(V.tensor_tensor(MK[:, b0:b1, :], MK[:, b0:b1, :], EL[:, b0:b1, :], ALU.add))
                for b in range(max(b0, 1), b1):
                    last = V.tensor_tensor(MR[:, b, :], MR[:, b - 1, :], MK[:, b - 1, :], ALU.add)
                    if b < b1 - 1:
                        link(last)
                last.then_inc(mk_done, 1)
                ve.wait_ge(mk_done, 1 if b0 == 0 else 2)

            link(V.memset(MR[:, 0, :], 0.0))
            route(0, 8, 4)
            hidden_low(1)
            route(8, NB, 5)
            hidden_low(2)
            ve.wait_ge(ps_pos, 1)
            mk_f, mr_f = (t[:, :, :].rearrange("p b e -> p (b e)") for t in (MK, MR))
            V.scalar_tensor_tensor(mr_f[:, 0:512], PS[:, 4, :], float(CAP), mk_f[:, 0:512], ALU.is_lt, ALU.mult)
            link(V.scalar_tensor_tensor(mr_f[:, 512:NB * NE], PS[:, 5, 0:NB * NE - 512], float(CAP),
                                        mk_f[:, 512:NB * NE], ALU.is_lt, ALU.mult))
            ve.wait_ge(el_done, NB)
            link(V.tensor_tensor(MR[:, :, :], MR[:, :, :], EL[:, :, :], ALU.mult))
            V.reciprocal(zsum[:, :], zsum[:, :])
            link(V.tensor_reduce(gate[:, :], MR[:, :, :], AX_X, ALU.add))
            link(V.tensor_tensor(gate[:, :], gate[:, :], zsum[:, :], ALU.mult))
            for b in range(NB):
                ve.wait_ge(y_ps, b + 1)
                V.scalar_tensor_tensor(ACC[:, b, :], PS[:, (1, 2, 3, 6, 7, 0)[b % 6], :], gate[:, b:b + 1], ACC[:, b, :],
                                       ALU.mult, ALU.add).then_inc(y_done, 1)

        @block.tensor
        def _(pe):
            MM = nc.tensor.matmul

            def product(out_t, pairs_t):
                steps = [(a[i], b[j]) for a, b in pairs_t for i, j in ((0, 0), (0, 1), (1, 0))]
                for s, (l, r) in enumerate(steps):
                    last = MM(out_t, l, r, start=s == 0, stop=s == len(steps) - 1)
                return last

            pe.wait_ge(const_done, 1)
            def transpose_x(b):
                pe.wait_ge(xn_ready, b + 1)
                if b >= 2:
                    pe.wait_ge(xt_lo, b - 1)
                for c in range(KC):
                    last = nc.tensor.transpose(PS[:, b % 2, c * P:(c + 1) * P], X[:, b, c * P:(c + 1) * P], ident[:, :])
                last.then_inc(xt_ps, 1)

            transpose_x(0)
            transpose_x(1)
            for b in range(NB):
                pe.wait_ge(xt_lo, b + 1)
                for n, (ready, used) in enumerate(((v_ps, v_biased), (h1_ps, h1_done))):
                    if b == 0:
                        pe.wait_ge(w_lo, n + 1)
                    if b >= 2:
                        pe.wait_ge(used, b - 1)
                    product(PS[:, 2 + 2 * n + b % 2, :], [([XT[l][:, c, blk(b)] for l in range(2)],
                                                           [WH[n][l][:, c, :] for l in range(2)])
                                                          for c in range(KC)]).then_inc(ready, 1)
                if b + 2 < NB:
                    transpose_x(b + 2)
                if b == NB - 3:
                    pe.wait_ge(etot_ready, NB)
                    MM(PS[:, 7, 0:NB], before[0:EP, :], e_tot[0:EP, :], start=True, stop=True)
                    MM(PS[:, 7, 64:64 + NB], ones_m[0:EP, :], e_tot[0:EP, :], start=True, stop=True).then_inc(epre_ready, 1)
            pe.wait_ge(v_biased, NB)

            def key_sums(j):
                pe.wait_ge(qk_act, NT * (j + 1))
                for b in range(NB):
                    g = 2 * NB * (j - NPAIR) + b
                    last = MM(PS[:, 6, g:g + NB + 1:NB], QF[j % 2][:, blk(b)], head_ones[:, DH - 1:DH + 1],
                              start=True, stop=True)
                if j == 2 * NPAIR - 1:
                    last.then_inc(ks_ps, 1)
                else:
                    last.then_inc(ks_read, 1)

            for j in range(2 * NPAIR):
                if j % NPAIR == 0:
                    pe.wait_ge(w_lo, 3 + j // NPAIR)
                wh = WH[j // NPAIR]
                for t, (c0, w) in enumerate(TILES):
                    n = NT * j + t
                    if n >= 4:
                        pe.wait_ge(qk_act, n - 3)
                    product(PS[:, n % 4, 0:w], [([wh[l][:, c, blk(j % NPAIR)] for l in range(2)],
                                                     [XT[l][:, c, c0:c0 + w] for l in range(2)])
                                                    for c in range(KC)]).then_inc(qk_ps, 1)
                if j > NPAIR:
                    key_sums(j - 1)
            key_sums(2 * NPAIR - 1)

            def first(p):
                return type(p) is int and p == 0

            def scores(p, i):
                s = i // NB
                if i % NB == 0:
                    pe.wait_ge(stack_in[s], (p + 1) * 80)
                if not (first(p) and i == 0):
                    pe.wait_ge(s_neg, p * (2 * NB) + i)
                for part in range(2):
                    for t, (c0, w) in enumerate(KTILES):
                        last = MM(PS[:, t, 0:w], QS[s][:, part, blk(i % NB)], KS[s][:, c0:c0 + w],
                                  start=part == 0, stop=part == 1)
                last.then_inc(s_ready, 1)

            def transposes(p, i):
                g = p * (2 * NB) + i
                if first(p) and i < 2:
                    pe.wait_ge(p_pad, i + 1)
                pe.wait_ge(p_exp, g + 1)
                for part, (b0, b1) in enumerate(PARTS):
                    if not (first(p) and i == 0):
                        pe.wait_ge(pt_lo, g * 2 - (1 - part))
                    for b in range(b0, b1):
                        last = nc.tensor.transpose(PS[:, 3 + b // 4, b % 4 * P:(b % 4 + 1) * P], PR[i % 2][:, blk(b)],
                                                   ident[:, :])
                    last.then_inc(pt_ps, 1)

            def values(p, k, half):
                if half == 0:
                    pe.wait_ge(pt_lo, p * (4 * NB) + 4 * (k + 1))
                    if not (first(p) and k < 2):
                        pe.wait_ge(o_out, p * NB + k - 1)
                for b in range(half * NB // 2, (half + 1) * NB // 2):
                    for part in range(2):
                        last = MM(PS[:, 6 + k % 2, 0:2 * P], VS[k // (NB // 2)][:, b, :], PT[k % 2][part][:, b, :],
                                  start=b == 0 and part == 0, stop=b == NB - 1 and part == 1)
                if half == 1:
                    last.then_inc(av_done, 1)

            def att_steps(p):
                for i in range(2 * NB):
                    scores(p, i)
                    if i > 0:
                        transposes(p, i - 1)
                    elif not first(p):
                        transposes(p - 1, 2 * NB - 1)
                    k, half = ((i - 3) // 2, 0) if i % 2 else ((i - 4) // 2, 1)
                    if k >= 0:
                        values(p, k, half)
                    elif not first(p):
                        values(p - 1, k + NB, half)

            att_steps(0)
            with pe.Fori(1, NPAIR) as p:
                att_steps(p)
            transposes(NPAIR - 1, 2 * NB - 1)
            values(NPAIR - 1, NB - 2, 1)
            values(NPAIR - 1, NB - 1, 0)
            values(NPAIR - 1, NB - 1, 1)

            pe.wait_ge(pt_lo, 2 * NG)
            pe.wait_ge(rinv_done, 1)
            for b in range(NB):
                last = nc.tensor.transpose(ps_flat[0:H, 3 * 512 + b * P:3 * 512 + (b + 1) * P], rowsum[:, b:NG:NB], ident[:, :])
            last.then_inc(rt_ps, 1)

            def spread_sums(t):
                c0, w = TILES[t]
                for p in range(NPAIR):
                    n = NPAIR * t + p
                    if n >= 3:
                        pe.wait_ge(on_f, n - 2)
                    MM(PS[:, n % 3, 0:w], head_rows[0:H, blk(p)], sums_t[:, c0:c0 + w], start=True, stop=True).then_inc(r_ps, 1)

            def project(b0, b1):
                for b in range(b0, b1):
                    pe.wait_ge(on_lo, NPAIR * (b // 4 + 1))
                    if b >= 4:
                        pe.wait_ge(acc_done, b - 3)
                    product(PS[:, 4 + b % 4, :], [([ON[l][:, c, blk(b)] for l in range(2)],
                                                   [WO[l][:, c, :] for l in range(2)]) for c in range(KC)]).then_inc(wo_ps, 1)

            pe.wait_ge(rt_done, 1)
            pe.wait_ge(head_rows_done, 1)
            spread_sums(0)
            spread_sums(1)
            pe.wait_ge(wo_lo, 1)
            pe.wait_ge(o_out, NG // 2)
            project(0, 2)
            spread_sums(2)
            project(2, NB)

            def counts(i, par, wait=True):
                if wait:
                    pe.wait_ge(ct_add, i + NB - 1)
                for j in range(4):
                    pe.wait_ge(oh_pool, i * 4 + (j + 1))
                    if j < 2:
                        pe.wait_ge(oh_dve, i * 2 + (j + 1))
                    else:
                        pe.wait_ge(oh_act, i * 2 + (j - 1))
                    for t, (c0, w) in enumerate(CTILES):
                        last = MM(PS[:, 4 * par + t, 0:w], OHD[par][:, j, :], OHS[4 * par + j][:, c0:c0 + w],
                                  start=j == 0, stop=j == 3)
                last.then_inc(ct_ps, 1)

            pe.wait_ge(acc_done, NB)
            pe.wait_ge(on_f, NPAIR * NT)
            with pe.Fori(0, NSC // 2) as k:
                counts(k * 2, 0)
                counts(k * 2 + 1, 1)

            pe.wait_ge(ct_add, NB + NSC)
            pe.wait_ge(dd_ready, 1)
            for b in range(NB):
                last = nc.tensor.transpose(ps_flat[0:1, 5 * 512 + b * P:5 * 512 + (b + 1) * P], dinv_half[:, b:b + 1],
                                           ident[:, :])
            last.then_inc(rt_ps, 1)
            pe.wait_ge(rt_done, 2)

            def spread_roots(t):
                c0, w = TILES[t]
                MM(PS[:, 6 + t % 2, 0:w], ones_m[0:1, :], roots_t[:, c0:c0 + w], start=True, stop=True).then_inc(dr_ps, 1)

            def agg1(n, b):
                c, (c0, w) = n // NT, TILES[n % NT]
                for l in range(2):
                    last = MM(PS[:, n % 8, 0:w], HS[l][:, b, c * P:(c + 1) * P], CTR[:, b, c0:c0 + w],
                              start=b == 0 and l == 0, stop=b == NB - 1 and l == 1)
                if b == NB - 1:
                    last.then_inc(g_ps, 1)

            for b in range(NB):
                pe.wait_ge(ct_ready, b + 1)
                pe.wait_ge(hs_lo, b + 1)
                for n in range(2 * NT):
                    agg1(n, b)
                if b == 0:
                    spread_roots(0)
                    spread_roots(1)
                if b == 2:
                    pe.wait_ge(dr_done, 1)
                    spread_roots(2)
            pe.wait_ge(dr_done, NT)
            for n in range(2 * NT, KC * NT):
                if n >= 8:
                    pe.wait_ge(g_done, n - 7)
                for b in range(NB):
                    agg1(n, b)

            def h2_part(b, c):
                for k, (i, j) in enumerate(((0, 0), (0, 1), (1, 0))):
                    last = MM(PS[:, (b + 4) % 8, :], GR[i][:, c, blk(b)], W2H[j][:, c, :],
                              start=c == 0 and k == 0, stop=c == KC - 1 and k == 2)
                if c == KC - 1:
                    last.then_inc(h2_ps, 1)

            pe.wait_ge(w2_lo, 1)
            pe.wait_ge(g_done, KC * NT - 3)
            for c in range(KC):
                pe.wait_ge(gr_lo, c + 1)
                for b in range(5):
                    h2_part(b, c)
            pe.wait_ge(g_done, KC * NT)
            for b in range(5, NB):
                if b >= 8:
                    pe.wait_ge(h2_b, b - 7)
                for c in range(KC):
                    h2_part(b, c)

            A2_BANKS = (6, 7, 0, 1)

            def agg2(b):
                if b < 4:
                    pe.wait_ge(h2_b, (3, 4, 5, 6)[b])
                else:
                    pe.wait_ge(x2_done, b - 3)
                for d in range(NB):
                    if b == 0:
                        pe.wait_ge(h2_lo, d + 1)
                    for l in range(2):
                        last = MM(PS[:, A2_BANKS[b % 4], :], CTR[:, d, blk(b)], H2[l][:, d, :],
                                  start=d == 0 and l == 0, stop=d == NB - 1 and l == 1)
                last.then_inc(a2_ps, 1)

            def transpose_x2(b):
                pe.wait_ge(xn2_ready, b + 1)
                if b >= 2:
                    pe.wait_ge(x2t_lo, b - 1)
                for c in range(KC):
                    last = nc.tensor.transpose(PS[:, 2 + b % 2, c * P:(c + 1) * P], XN[b % 4][:, c * P:(c + 1) * P],
                                               ident[:, :])
                last.then_inc(x2t_ps, 1)

            def logits(b):
                pe.wait_ge(x2t_lo, b + 1)
                if b == 0:
                    pe.wait_ge(f_lo, 3)
                product(PS[:, 4 + b // 8, b % 8 * NE:(b % 8 + 1) * NE],
                        [([X2T[l][:, c, blk(b)] for l in range(2)], [RW[l][:, c, :] for l in range(2)])
                         for c in range(KC)]).then_inc(lg_ps, 1)

            U_BANKS = (6, 7, 0)

            def hidden(t, f):
                n, (c0, w) = FC * t + f, TILES[t]
                pe.wait_ge(x2t_lo, (c0 + w) // P)
                if n >= 3:
                    pe.wait_ge(u_gelu, n - 2)
                else:
                    pe.wait_ge(x2_done, NB)
                product(PS[:, U_BANKS[n % 3], 0:w], [([F1[l][:, c, blk(f)] for l in range(2)],
                                                      [X2T[l][:, c, c0:c0 + w] for l in range(2)])
                                                     for c in range(KC)]).then_inc(u_ps, 1)

            Y_BANKS = (1, 2, 3, 6, 7, 0)

            def ffn_out(b):
                if b >= 6:
                    pe.wait_ge(y_done, b - 5)
                elif b >= 3:
                    pe.wait_ge(u_gelu, FC * NT)
                pe.wait_ge(u_lo, FC * (b // 4 + 1))
                pe.wait_ge(f_lo, 4)
                bank = PS[:, Y_BANKS[b % 6], :]
                for l in range(2):
                    MM(bank, ones_r[:, :], FB2[l][:, :], start=l == 0, stop=False)
                steps = [(HFH[i][:, f, blk(b)], F2[j][:, f, :]) for f in range(FC) for i, j in ((0, 0), (0, 1), (1, 0))]
                for k, (l, r) in enumerate(steps):
                    last = MM(bank, l, r, start=False, stop=k == len(steps) - 1)
                last.then_inc(y_ps, 1)

            for b in range(6):
                agg2(b)
            transpose_x2(0)
            transpose_x2(1)
            agg2(6)
            transpose_x2(2)
            transpose_x2(3)
            logits(0)
            logits(1)
            agg2(7)
            logits(2)
            logits(3)
            agg2(8)
            agg2(9)
            transpose_x2(4)
            transpose_x2(5)
            hidden(0, 0)
            transpose_x2(6)
            transpose_x2(7)
            hidden(0, 1)
            for b in range(4, 8):
                logits(b)
                if b < 6:
                    transpose_x2(b + 4)
            hidden(1, 0)
            logits(8)
            logits(9)
            hidden(1, 1)
            hidden(2, 0)
            hidden(2, 1)
            for b in range(3):
                ffn_out(b)
            pe.wait_ge(mk_done, 2)
            mk_f, mr_f = (t[:, :, :].rearrange("p b e -> p (b e)") for t in (MK, MR))
            for bank, c in ((4, slice(0, 512)), (5, slice(512, NB * NE))):
                w = c.stop - c.start
                MM(PS[:, bank, 0:w], before[:, :], mk_f[:, c], start=True, stop=False)
                last = MM(PS[:, bank, 0:w], ones_m[:, :], mr_f[:, c], start=False, stop=True)
            last.then_inc(ps_pos, 1)
            for b in range(3, NB):
                ffn_out(b)


_TRANSPOSED = {'L0_mix_Wq', 'L0_mix_Wk', 'L0_mix_Wv', 'L0_mix_Wo', 'L0_ffn_router_w', 'L0_ffn_w1', 'L0_ffn_w2'}
_INS = ['x', 'src', 'dst', 'L0_gnn_W1', 'L0_gnn_b1', 'L0_gnn_gamma', 'L0_gnn_beta', 'L0_gnn_W2', 'L0_gnn_b2',
        'L0_mix_Wq', 'L0_mix_bq', 'L0_mix_Wk', 'L0_mix_bk', 'L0_mix_Wv', 'L0_mix_bv', 'L0_mix_Wo', 'L0_mix_bo',
        'L0_ffn_router_w', 'L0_ffn_w1', 'L0_ffn_b1', 'L0_ffn_w2', 'L0_ffn_b2']


def kernel(**inputs):
    import numpy as _np
    import concourse.bacc as _bacc
    from concourse import mybir as _mybir
    from concourse.bass_utils import run_bass_kernel_spmd as _run

    nc = _bacc.Bacc("TRN2", target_bir_lowering=False, num_devices=1)
    arrays, args = {}, []
    for name in _INS:
        a = _np.asarray(inputs[name])
        a = _np.ascontiguousarray(a.T if name in _TRANSPOSED else a)
        arrays[f"in_{name}_dram"] = a
        args.append(nc.dram_tensor(f"in_{name}_dram", a.shape, _mybir.dt.from_np(a.dtype), kind="ExternalInput").ap())
    x = inputs['x']
    out = nc.dram_tensor("out_0_dram", x.shape, _mybir.dt.float32, kind="ExternalOutput").ap()
    gps_layer(nc, *args, out)
    r = _run(nc, [arrays], core_ids=[0])
    return r.results[0]["out_0_dram"]
```
